# Optimizing a Trainium2 kernel written in Bass

```python
import numpy as np
import jax
import jax.numpy as jnp

def _softmax(x, axis=-1):
    return jax.nn.softmax(x, axis=axis)

def _gelu(x):
    return jax.nn.gelu(x, approximate=True)

def _silu(x):
    return jax.nn.silu(x)

def _sigmoid(x):
    return jax.nn.sigmoid(x)

def _layernorm(x, axis=-1, eps=1e-05):
    m = jnp.mean(x, axis=axis, keepdims=True)
    v = jnp.var(x, axis=axis, keepdims=True)
    return (x - m) / jnp.sqrt(v + eps)

def _scatter_add(tgt, idx, src, axis=0):
    return tgt.at[idx].add(src)

def _segment_sum(src, seg, n):
    return jax.ops.segment_sum(src, seg, n)
kernel_name = 'mk_seq_preln_d1_jaxref_r2_4bee9c'

def setup_inputs(seed: int=0):
    np.random.seed(seed)
    _w = jnp.asarray

    def _L0_attn_setup():
        import jax, jax.numpy as jnp
        import numpy as np
        D_MODEL = 512
        D_STATE = 16
        D_CONV = 4
        EXPAND = 2
        CHUNK = 128
        D_INNER = D_MODEL * EXPAND
        BATCH = 2
        SEQLEN = 1024
        EPS = 1e-10
        LOG_CLAMP = 80.0

        def _forward(x, in_proj_w, conv_w, conv_b, x_proj_w, dt_w, dt_b, A_log, D_param, out_proj_w):
            Bsz, Lseq, _ = x.shape
            xz = x @ in_proj_w.T
            xi, z = jnp.split(xz, 2, axis=-1)
            xt = jnp.transpose(xi, (0, 2, 1))
            xt = jax.lax.conv_general_dilated(xt, conv_w, window_strides=(1,), padding=[(D_CONV - 1, 0)], dimension_numbers=('NCH', 'OIH', 'NCH'), feature_group_count=D_INNER) + conv_b[None, :, None]
            xc = jax.nn.silu(jnp.transpose(xt, (0, 2, 1)))
            xp = xc @ x_proj_w.T
            delta = jax.nn.softplus(xp[..., 0:1] * dt_w[:, 0] + dt_b)
            Bp = xp[..., 1:D_STATE + 1]
            Cp = xp[..., D_STATE + 1:]
            A = -jnp.exp(A_log)
            n_chunks = Lseq // CHUNK

            def resh(t):
                return jnp.transpose(t.reshape(Bsz, n_chunks, CHUNK, t.shape[-1]), (1, 0, 2, 3))
            xs = (resh(xc), resh(delta), resh(Bp), resh(Cp))
            h0 = jnp.zeros((Bsz, D_INNER, D_STATE), x.dtype)

            def step(h, inp):
                x_c, d_c, B_c, C_c = inp
                A_bar = jnp.exp(d_c[..., None] * A)
                BX = d_c[..., None] * B_c[:, :, None, :] * x_c[..., None]
                log_A_cum = jnp.cumsum(jnp.log(jnp.maximum(A_bar, EPS)), axis=1)
                A_cum = jnp.exp(jnp.minimum(log_A_cum, LOG_CLAMP))
                A_cum_sh = jnp.concatenate([jnp.ones_like(A_cum[:, :1]), A_cum[:, :-1]], axis=1)
                wcum = jnp.cumsum(BX / jnp.maximum(A_cum_sh, EPS), axis=1)
                h_chunk = A_cum * wcum / jnp.maximum(A_bar, EPS) + h[:, None] * A_cum
                y_c = jnp.einsum('bls,blds->bld', C_c, h_chunk) + D_param * x_c
                return (h_chunk[:, -1], y_c)
            _, ys = jax.lax.scan(step, h0, xs)
            y = jnp.transpose(ys, (1, 0, 2, 3)).reshape(Bsz, Lseq, D_INNER)
            y = y * jax.nn.silu(z)
            return y @ out_proj_w.T
        key = jax.random.key(seed)
        ks = jax.random.split(key, 7)
        s = 0.02
        x = jax.random.normal(ks[0], (BATCH, SEQLEN, D_MODEL), jnp.float32)
        in_proj_w = jax.random.normal(ks[1], (2 * D_INNER, D_MODEL), jnp.float32) * s
        conv_w = jax.random.normal(ks[2], (D_INNER, 1, D_CONV), jnp.float32) * 0.2
        conv_b = jnp.zeros((D_INNER,), jnp.float32)
        x_proj_w = jax.random.normal(ks[3], (2 * D_STATE + 1, D_INNER), jnp.float32) * s
        dt_w = jax.random.normal(ks[4], (D_INNER, 1), jnp.float32)
        dt_b = jax.random.normal(ks[5], (D_INNER,), jnp.float32) * 0.1
        A_log = jnp.log(jnp.arange(1, D_STATE + 1, dtype=jnp.float32))
        D_param = jnp.ones((D_INNER,), jnp.float32)
        out_proj_w = jax.random.normal(ks[6], (D_MODEL, D_INNER), jnp.float32) * s
        return {'x': x, 'in_proj_w': in_proj_w, 'conv_w': conv_w, 'conv_b': conv_b, 'x_proj_w': x_proj_w, 'dt_w': dt_w, 'dt_b': dt_b, 'A_log': A_log, 'D_param': D_param, 'out_proj_w': out_proj_w}
    _L0_attn_in = _L0_attn_setup()

    def _L0_ffn_setup():
        import jax, jax.numpy as jnp
        import numpy as np
        INT8_MAX = 127.0

        def _absmax_scale(x, axes):
            amax = jnp.max(jnp.abs(x), axis=axes, keepdims=True)
            return jnp.maximum(amax, 1e-12) / INT8_MAX
        key = jax.random.key(seed)
        k1, k2 = jax.random.split(key)
        lhs = jax.random.normal(k1, (4, 4096, 512), dtype=jnp.float32)
        rhs = jax.random.normal(k2, (512, 512), dtype=jnp.float32)
        return {'lhs': lhs, 'rhs': rhs}
    _L0_ffn_in = _L0_ffn_setup()
    _d = {'L0_attn_x': _L0_attn_in['x'], 'L0_attn_in_proj_w': _L0_attn_in['in_proj_w'], 'L0_attn_conv_w': _L0_attn_in['conv_w'], 'L0_attn_conv_b': _L0_attn_in['conv_b'], 'L0_attn_x_proj_w': _L0_attn_in['x_proj_w'], 'L0_attn_dt_w': _L0_attn_in['dt_w'], 'L0_attn_dt_b': _L0_attn_in['dt_b'], 'L0_attn_A_log': _L0_attn_in['A_log'], 'L0_attn_D_param': _L0_attn_in['D_param'], 'L0_attn_out_proj_w': _L0_attn_in['out_proj_w'], 'L0_ffn_rhs': _L0_ffn_in['rhs']}
    _x0 = _d['L0_attn_x']
    _d['L0_attn_x'] = jax.random.normal(jax.random.fold_in(jax.random.key(seed), 1), (8, 1024, 512), dtype=_x0.dtype)
    del _x0
    return _d

def reference(L0_attn_x, L0_attn_in_proj_w, L0_attn_conv_w, L0_attn_conv_b, L0_attn_x_proj_w, L0_attn_dt_w, L0_attn_dt_b, L0_attn_A_log, L0_attn_D_param, L0_attn_out_proj_w, L0_ffn_rhs):

    def _L0_attn_ref(x, in_proj_w, conv_w, conv_b, x_proj_w, dt_w, dt_b, A_log, D_param, out_proj_w):
        import jax, jax.numpy as jnp
        import numpy as np
        D_MODEL = 512
        D_STATE = 16
        D_CONV = 4
        EXPAND = 2
        CHUNK = 128
        D_INNER = D_MODEL * EXPAND
        BATCH = 2
        SEQLEN = 1024
        EPS = 1e-10
        LOG_CLAMP = 80.0

        def _forward(x, in_proj_w, conv_w, conv_b, x_proj_w, dt_w, dt_b, A_log, D_param, out_proj_w):
            Bsz, Lseq, _ = x.shape
            xz = x @ in_proj_w.T
            xi, z = jnp.split(xz, 2, axis=-1)
            xt = jnp.transpose(xi, (0, 2, 1))
            xt = jax.lax.conv_general_dilated(xt, conv_w, window_strides=(1,), padding=[(D_CONV - 1, 0)], dimension_numbers=('NCH', 'OIH', 'NCH'), feature_group_count=D_INNER) + conv_b[None, :, None]
            xc = jax.nn.silu(jnp.transpose(xt, (0, 2, 1)))
            xp = xc @ x_proj_w.T
            delta = jax.nn.softplus(xp[..., 0:1] * dt_w[:, 0] + dt_b)
            Bp = xp[..., 1:D_STATE + 1]
            Cp = xp[..., D_STATE + 1:]
            A = -jnp.exp(A_log)
            n_chunks = Lseq // CHUNK

            def resh(t):
                return jnp.transpose(t.reshape(Bsz, n_chunks, CHUNK, t.shape[-1]), (1, 0, 2, 3))
            xs = (resh(xc), resh(delta), resh(Bp), resh(Cp))
            h0 = jnp.zeros((Bsz, D_INNER, D_STATE), x.dtype)

            def step(h, inp):
                x_c, d_c, B_c, C_c = inp
                A_bar = jnp.exp(d_c[..., None] * A)
                BX = d_c[..., None] * B_c[:, :, None, :] * x_c[..., None]
                log_A_cum = jnp.cumsum(jnp.log(jnp.maximum(A_bar, EPS)), axis=1)
                A_cum = jnp.exp(jnp.minimum(log_A_cum, LOG_CLAMP))
                A_cum_sh = jnp.concatenate([jnp.ones_like(A_cum[:, :1]), A_cum[:, :-1]], axis=1)
                wcum = jnp.cumsum(BX / jnp.maximum(A_cum_sh, EPS), axis=1)
                h_chunk = A_cum * wcum / jnp.maximum(A_bar, EPS) + h[:, None] * A_cum
                y_c = jnp.einsum('bls,blds->bld', C_c, h_chunk) + D_param * x_c
                return (h_chunk[:, -1], y_c)
            _, ys = jax.lax.scan(step, h0, xs)
            y = jnp.transpose(ys, (1, 0, 2, 3)).reshape(Bsz, Lseq, D_INNER)
            y = y * jax.nn.silu(z)
            return y @ out_proj_w.T
        return _forward(x, in_proj_w, conv_w, conv_b, x_proj_w, dt_w, dt_b, A_log, D_param, out_proj_w)

    def _L0_ffn_ref(lhs, rhs):
        import jax, jax.numpy as jnp
        import numpy as np
        INT8_MAX = 127.0

        def _absmax_scale(x, axes):
            amax = jnp.max(jnp.abs(x), axis=axes, keepdims=True)
            return jnp.maximum(amax, 1e-12) / INT8_MAX
        lhs_scale = _absmax_scale(lhs, (2,))
        rhs_scale = _absmax_scale(rhs, (0,))
        q_lhs = jnp.clip(jnp.round(lhs / lhs_scale), -INT8_MAX, INT8_MAX).astype(jnp.int8)
        q_rhs = jnp.clip(jnp.round(rhs / rhs_scale), -INT8_MAX, INT8_MAX).astype(jnp.int8)
        acc = jax.lax.dot_general(q_lhs, q_rhs, (((2,), (0,)), ((), ())), preferred_element_type=jnp.int32)
        return acc.astype(jnp.float32) * lhs_scale * rhs_scale
    x = L0_attn_x
    x = x + _L0_attn_ref(_layernorm(x, axis=-1), L0_attn_in_proj_w, L0_attn_conv_w, L0_attn_conv_b, L0_attn_x_proj_w, L0_attn_dt_w, L0_attn_dt_b, L0_attn_A_log, L0_attn_D_param, L0_attn_out_proj_w)
    x = x + _L0_ffn_ref(_layernorm(x, axis=-1), L0_ffn_rhs)
    return x

_drawn_inputs = setup_inputs


def setup_inputs(seed=0):
    import zlib

    import numpy as np

    out = dict(_drawn_inputs(seed))
    spreads = {'L0_attn_conv_b': (0.0, 0.587), 'L0_attn_D_param': (1.0, 0.6)}
    factors = {'L0_attn_in_proj_w': 2.889,
     'L0_attn_conv_w': 3.083,
     'L0_attn_x_proj_w': 8.0,
     'L0_attn_dt_w': 8.0,
     'L0_attn_dt_b': 8.0,
     'L0_attn_A_log': 8.0,
     'L0_attn_out_proj_w': 2.746,
     'L0_ffn_rhs': 3.433}
    for name, (base, spread) in spreads.items():
        noise = np.random.default_rng([zlib.crc32(name.encode()), seed]).standard_normal(out[name].shape)
        drawn = base * np.exp(spread * noise) if base else spread * noise
        out[name] = jnp.asarray(drawn.astype(out[name].dtype))
    for name, factor in factors.items():
        out[name] = (out[name] * factor).astype(out[name].dtype)
    return out
```

```python
from contextlib import ExitStack

import numpy as np
import concourse.bass as bass
from concourse import mybir

F32 = mybir.dt.float32
BF16 = mybir.dt.bfloat16
U32 = mybir.dt.uint32
I32 = mybir.dt.int32
ALU = mybir.AluOpType
ACT = mybir.ActivationFunctionType
AX = mybir.AxisListType

P = 128
BATCH, SEQ, D = 8, 1024, 512
DI = 1024
NS = 16
TAPS = 4
KD, KI = D // P, DI // P
HALF = 512
CHUNKS = SEQ // P
TILES = BATCH * CHUNKS
PAIRS = TILES // 2
PARITY_ROWS = TILES // 2 * P
NPROJ = 2 * NS + 1
EPS = 1e-10
LN_EPS = float(np.log(np.float32(EPS)))
NORM_EPS = 1e-5
INT8_MAX = 127.0
RSQRT_MAGIC = 1597463007.0
ROUND = 12582912.0
SMALL = 2.0 ** -5
RING = 4
SLOTS = 32

FRONT_DVE = ("stats", "mean_var", "var_eps", "guess", "square1", "rstd1", "square2", "rstd2", "square3", "rstd3", "rstd",
             "xn", "halo_in", "tap3", "tap2",
             "tap1", "tap0", "halo_out", "b_rows", "c_rows", "c_last", "dt_lin", "dt_pos", "dt_negabs",
             "poly1", "poly2", "poly3", "poly4", "ct_keep", "small", "select", "delta", "dx")
FRONT_ACT = ("xnT", "xi0", "xi1", "xiT0", "xiT1", "z0", "z1", "xcT", "proj", "exp_dt",
             "xc0", "ln1p", "xc1", "ct")
FRONT_PE = ("xnT", "xi0", "xi1", "xiT0", "xiT1", "z0", "z1", "proj", "xc0", "xc1", "ct")
FRONT_POOL = ("skip",)
END_DVE = ("h", "habs", "hsel", "flag", "y0", "y1", "gate", "x2", "stats", "mean_var", "var_eps", "guess",
           "square1", "rstd1", "square2", "rstd2", "square3", "rstd3", "rstd", "xn2", "amax", "scale", "inv", "q_rounded", "q", "scaled", "out")
END_ACT = ("yT0", "yT1", "qT")
END_PE = ("flag", "fix0", "fix1", "yT0", "yT1", "attn", "qT", "ffn")


class Tile:

    def __init__(self, p, parity):
        self.p, self.parity = p, parity
        self.n = 2 * p + parity

    def shift(self, by):
        q = self.parity + by
        p = self.p + q // 2
        return None if isinstance(p, int) and p < 0 else Tile(p, q % 2)

    def row(self):
        return self.parity * PARITY_ROWS + self.p * P


def at(steps, tile, name):
    return tile.n * len(steps) + steps.index(name) + 1


def last_tile(tile):
    return isinstance(tile.n, int) and tile.n == TILES - 1


def slot_at(tile, slot, signals=1, slots=SLOTS):
    return tile.n * (slots * signals) + (slot + 1) * signals


def mamba_block(nc, x, w_in, conv_w, conv_b, w_x, dt_w, dt_b, a_log, d_skip, w_out, rhs_t, out):
    with ExitStack() as ctx:
        def sb(name, shape, dt=F32):
            return ctx.enter_context(nc.sbuf_tensor(name, shape, dt))

        def ps(name, shape, dt=F32):
            return ctx.enter_context(nc.psum_tensor(name, shape, dt))

        def sem(name):
            return ctx.enter_context(nc.semaphore(name))

        win = sb("win", [P, KD, 2 * DI])
        wout = sb("wout", [P, KI, D])
        wx = sb("wx", [P, KI, NPROJ])
        cw = sb("cw", [P, KI, TAPS])
        cb = sb("cb", [P, KI])
        dtw = sb("dtw", [P, DI])
        dtb = sb("dtb", [P, DI])
        dskip = sb("dskip", [P, DI])
        neg_a = sb("neg_a", [P, NS])
        ident = sb("ident", [P, P])
        ident_bf = sb("ident_bf", [P, P], BF16)
        tri_before = sb("tri_before", [P, P])
        tri_upto = sb("tri_upto", [P, P])
        ones = sb("ones", [P, P])
        not_last = sb("not_last", [P, 1])
        not_first = sb("not_first", [P, 1])
        keep = sb("keep", [P, PAIRS])
        rq = sb("rq", [P, KD, D], BF16)
        rscale = sb("rscale", [P, D])
        rcol = sb("rcol", [P, KD])
        rinv = sb("rinv", [P, KD])

        xt = sb("xt", [P, D])
        fstat = sb("fstat", [P, 6])
        fmv = sb("fmv", [P, 2])
        fsmall = sb("fsmall", [P, 6])
        xn = sb("xn", [P, D])
        xnT = sb("xnT", [P, KD, P])
        xi = sb("xi", [P, DI])
        xiT = sb("xiT", [P, KI, TAPS - 1 + P])
        xc = xiT[:, :, :].rearrange("p k t -> p (k t)")[:, 0:DI]
        halo = [sb(f"halo{i}", [P, KI, TAPS - 1]) for i in range(2)]
        conv = sb("conv", [P, KI, P])
        xcT = sb("xcT", [P, KI, P])
        proj = sb("proj", [P, NPROJ])
        clast = sb("clast", [P, NS])
        dt_a = sb("dt_a", [P, DI])
        dt_pos = sb("dt_pos", [P, DI])
        dt_y = xi
        dt_poly = conv[:, :, :].rearrange("p k t -> p (k t)")
        gate = [sb(f"gate{i}", [P, DI]) for i in range(2)]
        crow = [sb(f"crow{i}", [P, NS]) for i in range(2)]
        ct = [sb(f"ct{i}", [NS, 2, P]) for i in range(2)]
        ctk = [sb(f"ctk{i}", [NS, P]) for i in range(2)]
        brow = [sb(f"brow{i}", [P, NS]) for i in range(2)]
        bmat = [sb(f"bmat{i}", [P, P]) for i in range(2)]
        delta = [sb(f"delta{i}", [P, DI]) for i in range(2)]
        dx = [sb(f"dx{i}", [P, DI]) for i in range(2)]

        logdec = [sb(f"logdec{i}", [P, DI]) for i in range(2)]
        growths = sb("growths", [P, RING, DI])
        growth = [growths[:, i, :] for i in range(RING)]
        decay = [sb(f"decay{i}", [P, DI]) for i in range(RING)]
        source = growth
        term = [sb(f"term{i}", [P, DI]) for i in range(2)]
        acc = [sb(f"acc{i}", [P, DI]) for i in range(2)]
        hmain = sb("hmain", [NS, DI])
        hcarry = sb("hcarry", [NS, DI])
        hend = [sb(f"hend{i}", [NS, DI]) for i in range(2)]
        csel = sb("csel", [NS, 2, P])

        xres = sb("xres", [P, D])
        hm = sb("hm", [NS, 2])
        flag = sb("flag", [1, 2], I32)
        yg = dt_a
        ygT = dt_pos[:, :].rearrange("p (k t) -> p k t", t=P)
        x2 = sb("x2", [P, D])
        estat = sb("estat", [P, 6])
        emv = sb("emv", [P, 2])
        esmall = sb("esmall", [P, 8])
        xn2 = xn
        q_bf = sb("q_bf", [P, D], BF16)
        qT = sb("qT", [P, KD, P], BF16)
        res = xres
        rhs_sb = growths[:, 0:2, :].rearrange("p a (b n) -> p (a b) n", n=D)
        rq_rows = dt_a[:, :].bitcast(BF16).rearrange("p (k n) -> p k n", k=KD)

        cum = [ps(f"cum{i}", [P, DI]) for i in range(2)]
        state = [ps(f"state{i}", [P, HALF]) for i in range(2)]
        fbank = ps("fbank", [P, HALF])
        ebank = ps("ebank", [P, HALF])

        weights_loaded = sem("weights_loaded")
        consts_pool = sem("consts_pool")
        consts_dve = sem("consts_dve")
        consts_act = sem("consts_act")
        consts_pe = sem("consts_pe")
        x_loaded = sem("x_loaded")
        front_dve = sem("front_dve")
        front_act = sem("front_act")
        front_pe = sem("front_pe")
        front_pool = sem("front_pool")
        end_dve = sem("end_dve")
        end_act = sem("end_act")
        end_pe = sem("end_pe")
        hcarry_zeroed = sem("hcarry_zeroed")
        residual_loaded = sem("residual_loaded")
        out_stored = sem("out_stored")
        logdec_ready = sem("logdec_ready")
        cum_ready = sem("cum_ready")
        clamped = sem("clamped")
        growth_ready = sem("growth_ready")
        decay_ready = sem("decay_ready")
        source_ready = sem("source_ready")
        state_ready = sem("state_ready")
        term_ready = sem("term_ready")
        term_added = sem("term_added")
        last_saved = [sem(f"last_saved{i}") for i in range(2)]
        csel_ready = sem("csel_ready")
        stood = sem("stood")

        N_WEIGHTS = 11

        def saved_at(tile, slot):
            return 16 * (tile.n * (SLOTS // 2) + slot // 2 + 1)

        rdiags = [dt_y[:, j * P:(j + 1) * P] for j in range(KD)]

        def stand(eng):
            eng.sem_inc(stood, 1)

        def other_carries(eng, t):
            before = t.shift(-2)
            if before is None:
                eng.wait_ge(consts_pool, 1)
            else:
                eng.wait_ge(end_dve, at(END_DVE, before, "flag"))
            stand(eng)
            return eng.value_load(flag[0:1, t.parity:t.parity + 1], min_val=0, max_val=1)

        block = ctx.enter_context(nc.Block())

        def whole(tiles_of, front, body, end):
            front(Tile(0, 0))
            body(Tile(0, 0), True)
            body(Tile(0, 1), True)
            with tiles_of.Fori(1, PAIRS - 1) as p:
                body(Tile(p, 0), True)
                body(Tile(p, 1), True)
            body(Tile(PAIRS - 1, 0), True)
            body(Tile(PAIRS - 1, 1), False)
            end(Tile(PAIRS - 1, 1))

        @block.sync
        def _(sp):
            sp.dma_start(cw[:, :, :], conv_w.rearrange("(k p) t -> p k t", p=P)).then_inc(weights_loaded, 16)
            sp.dma_start(cb[:, :], conv_b).then_inc(weights_loaded, 16)
            sp.dma_start(neg_a[:, :], a_log.partition_broadcast(P)).then_inc(weights_loaded, 16)
            sp.dma_start(win[:, :, 0:DI], w_in.rearrange("(k p) e -> p k e", p=P)[:, :, 0:DI]).then_inc(weights_loaded, 16)
            sp.dma_start(win[:, :, DI:], w_in.rearrange("(k p) e -> p k e", p=P)[:, :, DI:]).then_inc(weights_loaded, 16)
            sp.dma_start(wx[:, :, :], w_x.rearrange("(k p) j -> p k j", p=P)).then_inc(weights_loaded, 16)
            sp.dma_start(dtw[:, :], dt_w.partition_broadcast(P)).then_inc(weights_loaded, 16)
            sp.dma_start(dtb[:, :], dt_b.partition_broadcast(P)).then_inc(weights_loaded, 16)
            sp.dma_start(dskip[:, :], d_skip.partition_broadcast(P)).then_inc(weights_loaded, 16)
            sp.dma_start(wout[:, :, :], w_out.rearrange("(k p) n -> p k n", p=P)).then_inc(weights_loaded, 16)
            sp.dma_start(rhs_sb, rhs_t.rearrange("(k p) n -> p k n", p=P)).then_inc(weights_loaded, 16)

            def load_x(t):
                before = t.shift(-1)
                if before is not None:
                    sp.wait_ge(front_dve, at(FRONT_DVE, before, "xn"))
                stand(sp)
                sp.dma_start(xt[:, :], x[bass.ds(t.row(), P), :]).then_inc(x_loaded, 16)

            def load_residual(t):
                before = t.shift(-1)
                if before is not None:
                    sp.wait_ge(out_stored, 16 * t.n)
                stand(sp)
                sp.dma_start(xres[:, :], x[bass.ds(t.row(), P), :]).then_inc(residual_loaded, 16)

            def store(t):
                sp.wait_ge(end_dve, at(END_DVE, t, "out"))
                stand(sp)
                sp.dma_start(out[bass.ds(t.row(), P), :], res[:, :]).then_inc(out_stored, 16)

            def save_last(t, slot):
                before = t.shift(-1)
                if slot == 0 and before is not None:
                    sp.wait_ge(end_dve, at(END_DVE, before, "h"))
                if slot == NS and before is not None:
                    sp.wait_ge(hcarry_zeroed, t.n + 1)
                if slot == NS and before is None:
                    sp.wait_ge(hcarry_zeroed, 1)
                if slot in (0, NS):
                    stand(sp)
                sp.wait_ge(term_ready, slot_at(t, slot, 2))
                rows = hmain if slot < NS else hcarry
                s = slot % NS
                sp.dma_start(rows[s:s + 1, :], term[slot % 2][P - 1:P, :]).then_inc(last_saved[slot % 2], 16)

            def body(t, more):
                prev = t.shift(-1)
                if prev is not None:
                    load_residual(prev)
                if more and not (isinstance(t.p, int) and t.p == PAIRS - 1):
                    load_x(t.shift(2))
                for s in range(NS):
                    save_last(t, s)
                    if s == 12 and prev is not None:
                        store(prev)
                save_last(t, NS)
                with sp.If(other_carries(sp, t)):
                    for slot in range(NS + 1, SLOTS):
                        save_last(t, slot)
                with sp.Else():
                    sp.wait_ge(last_saved[0], saved_at(t, NS))
                    sp.sem_inc(last_saved[0], 16 * 7)
                    sp.wait_ge(last_saved[1], saved_at(t, NS - 1))
                    sp.sem_inc(last_saved[1], 16 * 8)

            load_x(Tile(0, 0))
            load_x(Tile(0, 1))
            whole(sp, lambda t: None, body, lambda t: (load_residual(t), store(t)))
            sp.wait_ge(out_stored, 16 * TILES)

        @block.gpsimd
        def _(pool):
            nc.gpsimd.memset(flag[:, :], 0)
            nc.gpsimd.memset(ones[:, :], 1.0)
            nc.gpsimd.memset(ident[:, :], 0.0)
            nc.gpsimd.memset(hcarry[:, :], 0.0).then_inc(hcarry_zeroed, 1)
            for h in (*halo,):
                nc.gpsimd.memset(h[:, :, :], 0.0)
            for h in (*hend,):
                nc.gpsimd.memset(h[:, :], 0.0)
            nc.gpsimd.memset(keep[:, :], 1.0).then_inc(consts_pool, 1)
            pool.wait_ge(consts_pool, 1)
            nc.gpsimd.memset(keep[:, 0:PAIRS:CHUNKS], 0.0)
            nc.gpsimd.affine_select(out=ident[:, :], in_=ident[:, :], compare_op=ALU.not_equal, fill=1.0, base=0,
                                    pattern=[[-1, P]], channel_multiplier=1)
            nc.gpsimd.affine_select(out=tri_before[:, :], in_=ones[:, :], compare_op=ALU.is_gt, fill=0.0, base=0,
                                    pattern=[[1, P]], channel_multiplier=-1)
            nc.gpsimd.affine_select(out=tri_upto[:, :], in_=ones[:, :], compare_op=ALU.is_ge, fill=0.0, base=0,
                                    pattern=[[1, P]], channel_multiplier=-1).then_inc(consts_pool, 1)
            pool.wait_ge(consts_pool, 2)

            def front_skip(t):
                prev = t.shift(-2)
                pool.wait_ge(front_act, at(FRONT_ACT, t, "xc1"))
                if prev is not None:
                    pool.wait_ge(end_dve, at(END_DVE, prev, "y1"))
                nc.gpsimd.tensor_tensor(acc[t.parity][:, :], xc[:, :], dskip[:, :], ALU.mult).then_inc(front_pool, 1)

            def add(t, slot):
                pool.wait_ge(term_ready, slot_at(t, slot, 2))
                if slot == 0:
                    pool.wait_ge(front_pool, at(FRONT_POOL, t, "skip"))
                else:
                    pool.wait_ge(term_added, slot_at(t, slot - 1))
                a = acc[t.parity][:, :]
                nc.gpsimd.tensor_tensor(a, a, term[slot % 2][:, :], ALU.add).then_inc(term_added, 1)

            def body(t, more):
                prev = t.shift(-1)
                for s in range(NS):
                    add(t, s)
                    if s == 1 and prev is not None:
                        pool.wait_ge(end_dve, at(END_DVE, prev, "h"))
                        stand(pool)
                        nc.gpsimd.memset(hcarry[:, :], 0.0).then_inc(hcarry_zeroed, 1)
                    if s == 13 and more:
                        front_skip(t.shift(1))
                add(t, NS)
                with pool.If(other_carries(pool, t)):
                    for slot in range(NS + 1, SLOTS):
                        add(t, slot)
                with pool.Else():
                    pool.wait_ge(term_added, slot_at(t, NS))
                    pool.sem_inc(term_added, NS - 1)

            whole(pool, front_skip, body, lambda t: None)

        @block.scalar
        def _(act):
            act.wait_ge(weights_loaded, 16 * N_WEIGHTS)
            nc.scalar.activation(neg_a[:, :], neg_a[:, :], ACT.Exp).then_inc(consts_act, 1)
            for k in range(KD):
                act.wait_ge(consts_pe, k + 1)
                nc.scalar.activation(rq[:, k, :], fbank[:, 0:D // 2].bitcast(BF16), ACT.Copy).then_inc(consts_act, 1)
            act.wait_ge(consts_pe, KD + 1)
            nc.scalar.activation(rscale[:, :], ebank[:, :], ACT.Copy).then_inc(consts_act, 1)

            def evacuate(t, name, dst, src=None, func=ACT.Copy):
                act.wait_ge(front_pe, at(FRONT_PE, t, name))
                src = fbank[:, :] if src is None else src
                nc.scalar.activation(dst, src, func).then_inc(front_act, 1)

            blocks4 = fbank[:, :].rearrange("p (k t) -> p k t", t=P)

            def front_xnT(t):
                prev = t.shift(-1)
                if prev is not None:
                    act.wait_ge(front_pe, at(FRONT_PE, prev, "z1"))
                evacuate(t, "xnT", xnT[:, :, :], blocks4)

            def front_xi(t, h):
                prev = t.shift(-1)
                if prev is not None:
                    act.wait_ge(front_pe, at(FRONT_PE, prev, "xiT1"))
                    act.wait_ge(front_dve, at(FRONT_DVE, prev, "select"))
                evacuate(t, f"xi{h}", xi[:, h * HALF:(h + 1) * HALF])

            def front_xiT(t, h):
                prev = t.shift(-1)
                if prev is not None:
                    act.wait_ge(front_dve, at(FRONT_DVE, prev, "dx"))
                    act.wait_ge(front_pool, at(FRONT_POOL, prev, "skip"))
                evacuate(t, f"xiT{h}", xiT[:, 4 * h:4 * h + 4, TAPS - 1:], blocks4)

            def front_gate(t, h):
                prev = t.shift(-2)
                if prev is not None:
                    act.wait_ge(end_dve, at(END_DVE, prev, "gate"))
                evacuate(t, f"z{h}", gate[t.parity][:, h * HALF:(h + 1) * HALF], func=ACT.Silu)

            def front_xcT(t):
                prev = t.shift(-1)
                if prev is not None:
                    act.wait_ge(front_pe, at(FRONT_PE, prev, "xc1"))
                act.wait_ge(front_dve, at(FRONT_DVE, t, "tap0"))
                nc.scalar.activation(xcT[:, :, :], conv[:, :, :], ACT.Silu).then_inc(front_act, 1)

            def front_proj(t):
                prev = t.shift(-1)
                if prev is not None:
                    act.wait_ge(front_dve, at(FRONT_DVE, prev, "dt_lin"))
                evacuate(t, "proj", proj[:, :], fbank[:, 0:NPROJ])

            def front_xc(t, h):
                act.wait_ge(front_dve, at(FRONT_DVE, t, "halo_out"))
                evacuate(t, f"xc{h}", xc[:, h * HALF:(h + 1) * HALF])

            def front_ct(t):
                prev = t.shift(-2)
                if prev is not None:
                    act.wait_ge(end_pe, at(END_PE, prev, "fix1"))
                evacuate(t, "ct", ct[t.parity][:, :, :], fbank[0:NS, 0:2 * P].rearrange("s (a t) -> s a t", a=2))

            def front_exp_dt(t):
                act.wait_ge(front_dve, at(FRONT_DVE, t, "dt_negabs"))
                nc.scalar.activation(dt_y[:, :], dt_a[:, :], ACT.Exp).then_inc(front_act, 1)

            def front_ln1p(t):
                act.wait_ge(front_act, at(FRONT_ACT, t, "exp_dt"))
                nc.scalar.activation(dt_a[:, :], dt_y[:, :], ACT.Ln, bias=1.0).then_inc(front_act, 1)

            def end_yT(t, h):
                act.wait_ge(end_pe, at(END_PE, t, f"yT{h}"))
                ahead = t if last_tile(t) else t.shift(1)
                act.wait_ge(front_dve, at(FRONT_DVE, ahead, "delta"))
                nc.scalar.activation(ygT[:, 4 * h:4 * h + 4, :], ebank[:, :].rearrange("p (k t) -> p k t", t=P),
                                     ACT.Copy).then_inc(end_act, 1)

            def end_qT(t):
                act.wait_ge(end_pe, at(END_PE, t, "qT"))
                nc.scalar.activation(qT[:, :, :], ebank[:, 0:D // 2].bitcast(BF16).rearrange("p (k t) -> p k t", t=P),
                                     ACT.Copy).then_inc(end_act, 1)

            def exps(t, slot):
                act.wait_ge(cum_ready, slot_at(t, slot))
                c = cum[slot % 2][:, :]
                g = growth[slot % RING][:, :]
                if slot < NS:
                    if slot >= RING:
                        act.wait_ge(state_ready, slot_at(t, slot - RING, 2))
                    elif t.shift(-1) is not None:
                        act.wait_ge(state_ready, slot_at(t.shift(-1), NS - RING + slot, 2))
                    nc.scalar.activation(g, c, ACT.Relu, bias=-LN_EPS).then_inc(clamped, 1)
                if slot >= RING:
                    act.wait_ge(term_ready, slot_at(t, slot - RING, 2))
                elif t.shift(-1) is not None:
                    act.wait_ge(term_ready, slot_at(t.shift(-1), SLOTS - RING + slot, 2))
                nc.scalar.activation(decay[slot % RING][:, :], c, ACT.Exp).then_inc(decay_ready, 1)
                if slot < NS:
                    act.wait_ge(clamped, slot_at(t, slot, slots=NS))
                    nc.scalar.activation(g, g, ACT.Exp, scale=-1.0, bias=-LN_EPS).then_inc(growth_ready, 1)

            def front(t):
                front_xnT(t)
                front_xi(t, 0)
                front_xi(t, 1)
                front_xiT(t, 0)
                front_xiT(t, 1)
                front_gate(t, 0)
                front_gate(t, 1)
                front_xcT(t)
                front_proj(t)
                front_exp_dt(t)
                front_xc(t, 0)
                front_ln1p(t)
                front_xc(t, 1)
                front_ct(t)

            def body(t, more):
                prev, nxt = t.shift(-1), t.shift(1)
                exps(t, 0)
                exps(t, 1)
                for s in range(NS):
                    if s + 2 <= NS:
                        exps(t, s + 2)
                    if prev is not None:
                        if s == 4:
                            end_yT(prev, 0)
                        if s == 5:
                            end_yT(prev, 1)
                        if s == 10:
                            end_qT(prev)
                    if more:
                        if s == 1:
                            front_xnT(nxt)
                        if s == 2:
                            front_xi(nxt, 0)
                        if s == 3:
                            front_xi(nxt, 1)
                        if s == 4:
                            front_xiT(nxt, 0)
                        if s == 5:
                            front_xiT(nxt, 1)
                        if s == 7:
                            front_gate(nxt, 0)
                        if s == 9:
                            front_gate(nxt, 1)
                            front_xcT(nxt)
                        if s == 10:
                            front_proj(nxt)
                        if s == 11:
                            front_exp_dt(nxt)
                            front_xc(nxt, 0)
                            front_ln1p(nxt)
                        if s == 12:
                            front_xc(nxt, 1)
                        if s == 13:
                            front_ct(nxt)
                with act.If(other_carries(act, t)):
                    for slot in range(NS + 1, SLOTS):
                        exps(t, slot)
                with act.Else():
                    act.wait_ge(decay_ready, slot_at(t, NS))
                    act.sem_inc(decay_ready, NS - 1)

            def end(t):
                end_yT(t, 0)
                end_yT(t, 1)
                end_qT(t)

            whole(act, front, body, end)

        @block.tensor
        def _(pe):
            pe.wait_ge(consts_pool, 2)
            pe.wait_ge(consts_dve, 6)
            for k in range(KD):
                if k > 0:
                    pe.wait_ge(consts_act, k + 1)
                turned = fbank[:, 0:D // 2].bitcast(BF16)
                for j in range(KD):
                    last = nc.tensor.transpose(turned[:, j * P:(j + 1) * P], rq_rows[:, j, k * P:(k + 1) * P], ident_bf[:, :])
                last.then_inc(consts_pe, 1)
            for j in range(KD):
                pe.wait_ge(consts_dve, 7 + j)
                last = nc.tensor.matmul(ebank[:, j * P:(j + 1) * P], ones[:, :], rdiags[j], start=True, stop=True)
            last.then_inc(consts_pe, 1)
            pe.wait_ge(consts_act, KD + 2)

            def front_free(t, name):
                k = FRONT_PE.index(name)
                if k > 0:
                    pe.wait_ge(front_act, at(FRONT_ACT, t, FRONT_PE[k - 1]))
                elif t.shift(-1) is not None:
                    pe.wait_ge(front_act, at(FRONT_ACT, t.shift(-1), FRONT_PE[-1]))

            def turn4(t, name, src):
                front_free(t, name)
                for j in range(4):
                    last = nc.tensor.transpose(fbank[:, j * P:(j + 1) * P], src(j), ident[:, :])
                last.then_inc(front_pe, 1)

            def front_xnT(t):
                pe.wait_ge(front_dve, at(FRONT_DVE, t, "xn"))
                turn4(t, "xnT", lambda j: xn[:, j * P:(j + 1) * P])

            def front_in(t, name, col):
                pe.wait_ge(front_act, at(FRONT_ACT, t, "xnT"))
                front_free(t, name)
                for k in range(KD):
                    last = nc.tensor.matmul(fbank[:, :], xnT[:, k, :], win[:, k, col:col + HALF], start=(k == 0), stop=(k == KD - 1))
                last.then_inc(front_pe, 1)

            def front_xiT(t, h):
                pe.wait_ge(front_act, at(FRONT_ACT, t, "xi1"))
                turn4(t, f"xiT{h}", lambda j: xi[:, (4 * h + j) * P:(4 * h + j + 1) * P])

            def front_proj(t):
                pe.wait_ge(front_act, at(FRONT_ACT, t, "xcT"))
                front_free(t, "proj")
                for k in range(KI):
                    last = nc.tensor.matmul(fbank[:, 0:NPROJ], xcT[:, k, :], wx[:, k, :], start=(k == 0), stop=(k == KI - 1))
                last.then_inc(front_pe, 1)

            def front_xc(t, h):
                turn4(t, f"xc{h}", lambda j: xcT[:, 4 * h + j, :])

            def front_ct(t):
                front_free(t, "ct")
                pe.wait_ge(front_dve, at(FRONT_DVE, t, "c_last"))
                nc.tensor.transpose(fbank[0:NS, 0:P], crow[t.parity][:, :], ident[:, :])
                nc.tensor.transpose(fbank[0:NS, P:2 * P], clast[:, :], ident[:, :]).then_inc(front_pe, 1)

            emptied = {"flag": (end_dve, END_DVE, "flag"), "fix0": (end_dve, END_DVE, "y0"),
                       "fix1": (end_dve, END_DVE, "y1"), "yT0": (end_act, END_ACT, "yT0"),
                       "yT1": (end_act, END_ACT, "yT1"), "attn": (end_dve, END_DVE, "x2"),
                       "qT": (end_act, END_ACT, "qT"), "ffn": (end_dve, END_DVE, "scaled")}

            def end_free(t, name):
                k = END_PE.index(name)
                tile = t if k > 0 else t.shift(-1)
                if tile is not None:
                    s, steps, step = emptied[END_PE[k - 1]]
                    pe.wait_ge(s, at(steps, tile, step))

            def end_flag(t):
                pe.wait_ge(end_dve, at(END_DVE, t, "hsel"))
                end_free(t, "flag")
                stand(pe)
                nc.tensor.matmul(ebank[0:1, 0:1], hm[:, 1:2], ones[0:NS, 0:1], start=True, stop=True).then_inc(end_pe, 1)

            def end_fix(t, h):
                pe.wait_ge(end_dve, at(END_DVE, t, "h"))
                end_free(t, f"fix{h}")
                nc.tensor.matmul(ebank[:, :], ct[t.parity][:, 1, :], hend[t.parity][:, h * HALF:(h + 1) * HALF],
                                 start=True, stop=True).then_inc(end_pe, 1)

            def end_yT(t, h):
                pe.wait_ge(end_dve, at(END_DVE, t, "gate"))
                end_free(t, f"yT{h}")
                for j in range(4):
                    last = nc.tensor.transpose(ebank[:, j * P:(j + 1) * P], yg[:, (4 * h + j) * P:(4 * h + j + 1) * P], ident[:, :])
                last.then_inc(end_pe, 1)

            def end_attn(t):
                end_free(t, "attn")
                for k in range(KI):
                    last = nc.tensor.matmul(ebank[:, :], ygT[:, k, :], wout[:, k, :], start=(k == 0), stop=(k == KI - 1))
                last.then_inc(end_pe, 1)

            def end_qT(t):
                pe.wait_ge(end_dve, at(END_DVE, t, "q"))
                end_free(t, "qT")
                turned = ebank[:, 0:D // 2].bitcast(BF16)
                for j in range(KD):
                    last = nc.tensor.transpose(turned[:, j * P:(j + 1) * P], q_bf[:, j * P:(j + 1) * P], ident_bf[:, :])
                last.then_inc(end_pe, 1)

            def end_ffn(t):
                end_free(t, "ffn")
                for k in range(KD):
                    last = nc.tensor.matmul(ebank[:, :], qT[:, k, :], rq[:, k, :], start=(k == 0), stop=(k == KD - 1))
                last.then_inc(end_pe, 1)

            def cumulate(t, slot):
                pe.wait_ge(logdec_ready, slot_at(t, slot))
                if slot >= 2:
                    pe.wait_ge(decay_ready, slot_at(t, slot - 2))
                elif t.shift(-1) is not None:
                    pe.wait_ge(decay_ready, slot_at(t.shift(-1), SLOTS - 2 + slot))
                tri = tri_before if slot < NS else tri_upto
                for h in range(2):
                    cols = slice(h * HALF, (h + 1) * HALF)
                    last = nc.tensor.matmul(cum[slot % 2][:, cols], tri[:, :], logdec[slot % 2][:, cols], start=True, stop=True)
                last.then_inc(cum_ready, 1)

            def state_free(t, slot, h):
                if slot > 0:
                    pe.wait_ge(term_ready, slot_at(t, slot - 1, 2) - 1 + h)
                elif t.shift(-1) is not None:
                    pe.wait_ge(term_ready, slot_at(t.shift(-1), SLOTS - 1, 2) - 1 + h)

            def states(t, s):
                pe.wait_ge(source_ready, slot_at(t, s, slots=NS))
                for h in range(2):
                    state_free(t, s, h)
                    nc.tensor.matmul(state[h][:, :], bmat[s % 2][:, :], source[s % RING][:, h * HALF:(h + 1) * HALF],
                                     start=True, stop=True).then_inc(state_ready, 1)

            def carries(t, slot):
                s = slot - NS
                before = t.shift(-2)
                if s == 0:
                    pe.wait_ge(front_dve, at(FRONT_DVE, t, "ct_keep"))
                    if before is not None:
                        pe.wait_ge(end_dve, at(END_DVE, before, "h"))
                for h in range(2):
                    state_free(t, slot, h)
                    cols = slice(h * HALF, (h + 1) * HALF)
                    if s == 0:
                        nc.tensor.matmul(state[h][:, :], ctk[t.parity][0:1, :], hend[t.parity][0:1, cols], start=True, stop=True)\
                            .then_inc(state_ready, 1)
                    else:
                        if h == 0:
                            pe.wait_ge(csel_ready, t.n * (NS - 1) + s)
                        nc.tensor.matmul(state[h][:, :], csel[:, s % 2, :], hend[t.parity][:, cols], start=True, stop=True)\
                            .then_inc(state_ready, 1)

            def front(t):
                front_xnT(t)
                front_in(t, "xi0", 0)
                front_in(t, "xi1", HALF)
                front_xiT(t, 0)
                front_xiT(t, 1)
                front_in(t, "z0", DI)
                front_in(t, "z1", DI + HALF)
                front_proj(t)
                front_xc(t, 0)
                front_xc(t, 1)
                front_ct(t)

            def body(t, more):
                prev, nxt = t.shift(-1), t.shift(1)
                cumulate(t, 0)
                cumulate(t, 1)
                for s in range(NS):
                    if s + 2 <= NS:
                        cumulate(t, s + 2)
                    if more:
                        if s == 2:
                            front_in(nxt, "xi0", 0)
                        if s == 3:
                            front_in(nxt, "xi1", HALF)
                        if s == 4:
                            front_xiT(nxt, 0)
                        if s == 5:
                            front_xiT(nxt, 1)
                        if s == 7:
                            front_in(nxt, "z0", DI)
                        if s == 8:
                            front_in(nxt, "z1", DI + HALF)
                        if s == 10:
                            front_proj(nxt)
                    if prev is not None:
                        if s == 4:
                            end_yT(prev, 0)
                        if s == 5:
                            end_yT(prev, 1)
                        if s == 6:
                            end_attn(prev)
                        if s == 10:
                            end_qT(prev)
                        if s == 11:
                            end_ffn(prev)
                    states(t, s)
                    if more:
                        if s == 1:
                            front_xnT(nxt)
                        if s == 10:
                            front_xc(nxt, 0)
                        if s == 11:
                            front_xc(nxt, 1)
                        if s == 12:
                            front_ct(nxt)
                    if prev is not None:
                        if s == 0:
                            end_flag(prev)
                        if s == 1:
                            end_fix(prev, 0)
                        if s == 2:
                            end_fix(prev, 1)
                carries(t, NS)
                with pe.If(other_carries(pe, t)):
                    for slot in range(NS + 1, SLOTS):
                        cumulate(t, slot)
                        carries(t, slot)
                with pe.Else():
                    pe.wait_ge(cum_ready, slot_at(t, NS))
                    pe.sem_inc(cum_ready, NS - 1)
                    pe.wait_ge(state_ready, slot_at(t, NS, 2))
                    pe.sem_inc(state_ready, 2 * (NS - 1))

            def end(t):
                end_flag(t)
                end_fix(t, 0)
                end_fix(t, 1)
                end_yT(t, 0)
                end_yT(t, 1)
                end_attn(t)
                end_qT(t)
                end_ffn(t)

            whole(pe, front, body, end)

        @block.vector
        def _(dve):
            def done(ins, s, value):
                ins.then_inc(s, 1)
                dve.wait_ge(s, value)

            dve.wait_ge(consts_pool, 2)
            dve.wait_ge(weights_loaded, 16 * N_WEIGHTS)
            nc.vector.tensor_copy(ident_bf[:, :], ident[:, :])
            nc.vector.tensor_scalar(not_last[:, :], ident[:, P - 1:P], -1.0, 1.0, ALU.mult, ALU.add)
            nc.vector.tensor_scalar(not_first[:, :], ident[:, 0:1], -1.0, 1.0, ALU.mult, ALU.add)
            done(nc.vector.tensor_reduce(rcol[:, :], rhs_sb, AX.X, ALU.max, apply_absolute_value=True), consts_dve, 1)
            done(nc.vector.tensor_scalar(rcol[:, :], rcol[:, :], 1e-12, 1.0 / INT8_MAX, ALU.max, ALU.mult), consts_dve, 2)
            done(nc.vector.reciprocal(rinv[:, :], rcol[:, :]), consts_dve, 3)
            for k in range(KD):
                nc.vector.tensor_scalar(rhs_sb[:, k, :], rhs_sb[:, k, :], rinv[:, k:k + 1], ROUND, ALU.mult, ALU.add)
            nc.vector.tensor_scalar(yg[:, 0:1], ones[:, 0:1], 0.0, None, ALU.mult).then_inc(consts_dve, 1)
            dve.wait_ge(consts_dve, 4)
            nc.vector.tensor_scalar(rq_rows, rhs_sb, -ROUND, None, ALU.add).then_inc(consts_dve, 1)
            dve.wait_ge(consts_act, 1)
            nc.vector.tensor_scalar(neg_a[:, :], neg_a[:, :], -1.0, None, ALU.mult).then_inc(consts_dve, 1)
            for j in range(KD):
                if j < KD - 1:
                    nc.vector.tensor_scalar(rdiags[j], ident[:, :], rcol[:, j:j + 1], None, ALU.mult).then_inc(consts_dve, 1)
                else:
                    nc.vector.tensor_scalar(rdiags[j], ident[:, :], rcol[:, j:j + 1], None, ALU.mult).then_inc(consts_dve, 1)
            dve.wait_ge(consts_act, KD + 2)

            def moments(t, src, stats, mv, small, s, steps):
                done(nc.vector.bn_stats(stats[:, :], src), s, at(steps, t, "stats"))
                stand(dve)
                done(nc.vector.bn_aggr(mv[:, :], stats[:, :]), s, at(steps, t, "mean_var"))
                done(nc.vector.tensor_scalar(small[:, 0:1], mv[:, 1:2], NORM_EPS, None, ALU.add), s, at(steps, t, "var_eps"))

            def norm(t, src, mv, small, dst, s, steps):
                v = small[:, 0:1]
                done(nc.vector.tensor_scalar(small[:, 1:2].bitcast(I32), v.bitcast(I32), -0.5, RSQRT_MAGIC, ALU.mult, ALU.add),
                     s, at(steps, t, "guess"))
                r, c = small[:, 1:2], 1.0
                for k in (1, 2, 3):
                    done(nc.vector.scalar_tensor_tensor(out=small[:, 2:3], in0=r, scalar=v, in1=r, op0=ALU.mult, op1=ALU.mult),
                         s, at(steps, t, f"square{k}"))
                    done(nc.vector.scalar_tensor_tensor(out=r, in0=small[:, 2:3], scalar=-3.0 * c * c, in1=r, op0=ALU.add,
                                                        op1=ALU.mult), s, at(steps, t, f"rstd{k}"))
                    c = -2.0 * c ** 3
                done(nc.vector.tensor_scalar(small[:, 3:4], r, 1.0 / c, None, ALU.mult), s, at(steps, t, "rstd"))
                nc.vector.tensor_scalar(dst, src, mv[:, 0:1], small[:, 3:4], ALU.subtract, ALU.mult).then_inc(s, 1)

            def front_moments(t):
                dve.wait_ge(x_loaded, 16 * (t.n + 1))
                moments(t, xt[:, :], fstat, fmv, fsmall, front_dve, FRONT_DVE)

            def front_norm(t):
                if t.shift(-1) is not None:
                    dve.wait_ge(front_pe, at(FRONT_PE, t.shift(-1), "xnT"))
                if t.shift(-3) is not None:
                    dve.wait_ge(end_dve, at(END_DVE, t.shift(-3), "q"))
                norm(t, xt[:, :], fmv, fsmall, xn[:, :], front_dve, FRONT_DVE)

            def front_halo(t):
                if t.shift(-1) is not None:
                    dve.wait_ge(front_dve, at(FRONT_DVE, t.shift(-1), "dx"))
                    dve.wait_ge(front_pool, at(FRONT_POOL, t.shift(-1), "skip"))
                nc.vector.tensor_scalar(xiT[:, :, 0:TAPS - 1], halo[t.parity][:, :, :], keep[:, bass.ds(t.p, 1)], None,
                                        ALU.mult).then_inc(front_dve, 1)

            def front_conv(t, tap):
                if tap == TAPS - 1:
                    dve.wait_ge(front_act, at(FRONT_ACT, t, "xiT1"))
                    if t.shift(-1) is not None:
                        dve.wait_ge(front_act, at(FRONT_ACT, t.shift(-1), "xcT"))
                else:
                    dve.wait_ge(front_dve, at(FRONT_DVE, t, f"tap{tap + 1}"))
                for k in range(KI):
                    src, w = xiT[:, k, tap:tap + P], cw[:, k, tap:tap + 1]
                    if tap == TAPS - 1:
                        last = nc.vector.tensor_scalar(conv[:, k, :], src, w, cb[:, k:k + 1], ALU.mult, ALU.add)
                    else:
                        last = nc.vector.scalar_tensor_tensor(out=conv[:, k, :], in0=src, scalar=w, in1=conv[:, k, :],
                                                              op0=ALU.mult, op1=ALU.add)
                last.then_inc(front_dve, 1)
                if tap == 0:
                    nc.vector.tensor_copy(halo[t.parity][:, :, :], xiT[:, :, P:]).then_inc(front_dve, 1)

            def front_c(t):
                dve.wait_ge(front_act, at(FRONT_ACT, t, "proj"))
                if t.shift(-2) is not None:
                    dve.wait_ge(term_ready, slot_at(t.shift(-2), NS - 1, 2))
                    dve.wait_ge(front_pe, at(FRONT_PE, t.shift(-1), "ct"))
                elif t.shift(-1) is not None:
                    dve.wait_ge(front_pe, at(FRONT_PE, t.shift(-1), "ct"))
                nc.vector.tensor_copy(brow[t.parity][:, :], proj[:, 1:1 + NS]).then_inc(front_dve, 1)
                last_row = ident[:, P - 1:P]
                c = proj[:, 1 + NS:NPROJ]
                nc.vector.tensor_scalar(crow[t.parity][:, :], c, not_last[:, :], last_row, ALU.mult, ALU.add).then_inc(front_dve, 1)
                nc.vector.tensor_scalar(clast[:, :], c, 1.0, last_row, ALU.subtract, ALU.mult).then_inc(front_dve, 1)

            def front_ct_keep(t):
                dve.wait_ge(front_act, at(FRONT_ACT, t, "ct"))
                if t.shift(-2) is not None:
                    dve.wait_ge(state_ready, slot_at(t.shift(-2), SLOTS - 1, 2))
                nc.vector.tensor_scalar(ctk[t.parity][:, :], ct[t.parity][:, 0, :], keep[0:NS, bass.ds(t.p, 1)], None,
                                        ALU.mult).then_inc(front_dve, 1)

            def front_dt(t):
                if t.shift(-2) is not None:
                    dve.wait_ge(end_pe, at(END_PE, t.shift(-2), "attn"))
                done(nc.vector.scalar_tensor_tensor(out=dt_a[:, :], in0=dtw[:, :], scalar=proj[:, 0:1], in1=dtb[:, :],
                                                    op0=ALU.mult, op1=ALU.add), front_dve, at(FRONT_DVE, t, "dt_lin"))
                done(nc.vector.tensor_scalar(dt_pos[:, :], dt_a[:, :], 0.0, None, ALU.max), front_dve, at(FRONT_DVE, t, "dt_pos"))
                nc.vector.scalar_tensor_tensor(out=dt_a[:, :], in0=dt_pos[:, :], scalar=-2.0, in1=dt_a[:, :],
                                               op0=ALU.mult, op1=ALU.add).then_inc(front_dve, 1)

            def front_poly(t, half):
                y, r = dt_y[:, :], dt_poly[:, :]
                if half == 0:
                    dve.wait_ge(front_act, at(FRONT_ACT, t, "exp_dt"))
                    done(nc.vector.tensor_scalar(r, y, -0.25, 1.0 / 3.0, ALU.mult, ALU.add), front_dve, at(FRONT_DVE, t, "poly1"))
                    nc.vector.tensor_tensor(r, r, y, ALU.mult).then_inc(front_dve, 1)
                else:
                    dve.wait_ge(front_dve, at(FRONT_DVE, t, "poly2"))
                    done(nc.vector.scalar_tensor_tensor(out=r, in0=r, scalar=-0.5, in1=y, op0=ALU.add, op1=ALU.mult),
                         front_dve, at(FRONT_DVE, t, "poly3"))
                    nc.vector.scalar_tensor_tensor(out=r, in0=r, scalar=1.0, in1=y, op0=ALU.add, op1=ALU.mult).then_inc(front_dve, 1)

            def front_delta(t):
                dve.wait_ge(front_act, at(FRONT_ACT, t, "ln1p"))
                mask = dt_y[:, :].bitcast(U32)
                nc.vector.tensor_scalar(mask, dt_y[:, :], SMALL, None, ALU.is_lt).then_inc(front_dve, 1)
                dve.wait_ge(front_dve, at(FRONT_DVE, t, "small"))
                stand(dve)
                done(nc.vector.copy_predicated(dt_a[:, :], mask, dt_poly[:, :]), front_dve, at(FRONT_DVE, t, "select"))
                if t.shift(-2) is not None:
                    dve.wait_ge(logdec_ready, slot_at(t.shift(-2), SLOTS - 1))
                done(nc.vector.tensor_tensor(delta[t.parity][:, :], dt_a[:, :], dt_pos[:, :], ALU.add),
                     front_dve, at(FRONT_DVE, t, "delta"))

            def front_dx(t):
                dve.wait_ge(front_act, at(FRONT_ACT, t, "xc1"))
                if t.shift(-2) is not None:
                    dve.wait_ge(source_ready, slot_at(t.shift(-2), NS - 1, slots=NS))
                nc.vector.tensor_tensor(dx[t.parity][:, :], delta[t.parity][:, :], xc[:, :], ALU.mult).then_inc(front_dve, 1)

            def end_h(t):
                before = t.shift(-1)
                for k in range(2):
                    dve.wait_ge(last_saved[k], saved_at(t, SLOTS - 2 + k))
                dve.wait_ge(state_ready, slot_at(t, SLOTS - 1, 2))
                if before is not None:
                    dve.wait_ge(end_pe, at(END_PE, before, "fix1"))
                h = hend[t.parity][:, :]
                done(nc.vector.tensor_tensor(h, hmain[:, :], hcarry[:, :], ALU.add), end_dve, at(END_DVE, t, "h"))
                done(nc.vector.tensor_reduce(hm[:, 0:1], h, AX.X, ALU.max, apply_absolute_value=True), end_dve, at(END_DVE, t, "habs"))
                nc.vector.tensor_scalar(hm[:, 1:2], hm[:, 0:1], not_first[0:NS, :], None, ALU.mult).then_inc(end_dve, 1)

            def end_flag(t):
                if last_tile(t):
                    dve.wait_ge(term_added, slot_at(t, SLOTS - 1))
                    dve.wait_ge(decay_ready, slot_at(t, SLOTS - 1))
                dve.wait_ge(end_pe, at(END_PE, t, "flag"))
                after = keep[0:1, bass.ds(t.p + 1, 1)] if not (isinstance(t.p, int) and t.p == PAIRS - 1) else keep[0:1, 0:1]
                nc.vector.tensor_scalar(flag[0:1, t.parity:t.parity + 1], ebank[0:1, 0:1], after, 0.0, ALU.mult, ALU.is_gt)\
                    .then_inc(end_dve, 1)

            def end_y(t, h):
                cols = slice(h * HALF, (h + 1) * HALF)
                dve.wait_ge(term_added, slot_at(t, SLOTS - 1))
                dve.wait_ge(front_dve, at(FRONT_DVE, t if last_tile(t) else t.shift(1), "delta"))
                dve.wait_ge(end_pe, at(END_PE, t, f"fix{h}"))
                nc.vector.tensor_tensor(yg[:, cols], ebank[:, :], acc[t.parity][:, cols], ALU.add).then_inc(end_dve, 1)

            def end_gate(t):
                dve.wait_ge(end_dve, at(END_DVE, t, "y1"))
                nc.vector.tensor_tensor(yg[:, :], yg[:, :], gate[t.parity][:, :], ALU.mult).then_inc(end_dve, 1)

            def end_moments(t):
                dve.wait_ge(end_pe, at(END_PE, t, "attn"))
                dve.wait_ge(residual_loaded, 16 * (t.n + 1))
                if t.shift(-1) is not None:
                    dve.wait_ge(end_dve, at(END_DVE, t.shift(-1), "out"))
                done(nc.vector.tensor_tensor(x2[:, :], ebank[:, :], xres[:, :], ALU.add), end_dve, at(END_DVE, t, "x2"))
                moments(t, x2[:, :], estat, emv, esmall, end_dve, END_DVE)

            def end_norm(t):
                if not last_tile(t) and not last_tile(t.shift(1)):
                    dve.wait_ge(front_pe, at(FRONT_PE, t.shift(2), "xnT"))
                norm(t, x2[:, :], emv, esmall, xn2[:, :], end_dve, END_DVE)

            def end_quantise(t):
                dve.wait_ge(end_dve, at(END_DVE, t, "xn2"))
                done(nc.vector.tensor_reduce(esmall[:, 6:7], xn2[:, :], AX.X, ALU.max, apply_absolute_value=True),
                     end_dve, at(END_DVE, t, "amax"))
                done(nc.vector.tensor_scalar(esmall[:, 6:7], esmall[:, 6:7], 1e-12, 1.0 / INT8_MAX, ALU.max, ALU.mult),
                     end_dve, at(END_DVE, t, "scale"))
                done(nc.vector.reciprocal(esmall[:, 7:8], esmall[:, 6:7]), end_dve, at(END_DVE, t, "inv"))
                done(nc.vector.tensor_scalar(xn2[:, :], xn2[:, :], esmall[:, 7:8], ROUND, ALU.mult, ALU.add),
                     end_dve, at(END_DVE, t, "q_rounded"))
                if t.shift(-1) is not None:
                    dve.wait_ge(end_pe, at(END_PE, t.shift(-1), "qT"))
                nc.vector.tensor_scalar(q_bf[:, :], xn2[:, :], -ROUND, None, ALU.add).then_inc(end_dve, 1)

            def end_out(t):
                dve.wait_ge(end_pe, at(END_PE, t, "ffn"))
                if t.shift(-1) is not None:
                    dve.wait_ge(out_stored, 16 * t.n)
                done(nc.vector.scalar_tensor_tensor(out=res[:, :], in0=ebank[:, :], scalar=esmall[:, 6:7], in1=rscale[:, :],
                                                    op0=ALU.mult, op1=ALU.mult), end_dve, at(END_DVE, t, "scaled"))
                nc.vector.tensor_tensor(res[:, :], res[:, :], x2[:, :], ALU.add).then_inc(end_dve, 1)

            def log_decay(t, slot):
                if slot == 0:
                    dve.wait_ge(front_dve, at(FRONT_DVE, t, "delta"))
                if slot >= 2:
                    dve.wait_ge(cum_ready, slot_at(t, slot - 2))
                elif t.shift(-1) is not None:
                    dve.wait_ge(cum_ready, slot_at(t.shift(-1), SLOTS - 2 + slot))
                s = slot % NS
                nc.vector.tensor_scalar(logdec[slot % 2][:, :], delta[t.parity][:, :], neg_a[:, s:s + 1], LN_EPS,
                                        ALU.mult, ALU.max).then_inc(logdec_ready, 1)

            def source_of(t, s):
                if s == 0:
                    dve.wait_ge(front_dve, at(FRONT_DVE, t, "dx"))
                dve.wait_ge(growth_ready, slot_at(t, s, slots=NS))
                g = growth[s % RING][:, :]
                if s >= 2:
                    dve.wait_ge(state_ready, slot_at(t, s - 2, 2))
                elif t.shift(-1) is not None:
                    dve.wait_ge(state_ready, slot_at(t.shift(-1), NS - 2 + s, 2))
                nc.vector.tensor_scalar(bmat[s % 2][:, :], tri_upto[:, :], brow[t.parity][:, s:s + 1], None, ALU.mult)
                nc.vector.tensor_tensor(g, g, dx[t.parity][:, :], ALU.mult).then_inc(source_ready, 1)

            def term_of(t, slot):
                before, old = (t, slot - 2) if slot >= 2 else (t.shift(-1), SLOTS - 2 + slot)
                if before is not None:
                    dve.wait_ge(term_added, slot_at(before, old))
                    dve.wait_ge(last_saved[slot % 2], saved_at(before, old))
                dve.wait_ge(decay_ready, slot_at(t, slot))
                for h in range(2):
                    cols = slice(h * HALF, (h + 1) * HALF)
                    dve.wait_ge(state_ready, slot_at(t, slot, 2) - 1 + h)
                    if slot < NS:
                        nc.vector.scalar_tensor_tensor(out=term[slot % 2][:, cols], in0=state[h][:, :],
                                                       scalar=crow[t.parity][:, slot:slot + 1], in1=decay[slot % RING][:, cols],
                                                       op0=ALU.mult, op1=ALU.mult).then_inc(term_ready, 1)
                    else:
                        nc.vector.tensor_tensor(term[slot % 2][:, cols], state[h][:, :], decay[slot % RING][:, cols],
                                                ALU.mult).then_inc(term_ready, 1)

            def front(t):
                front_moments(t)
                front_norm(t)
                front_halo(t)
                for tap in range(TAPS - 1, -1, -1):
                    front_conv(t, tap)
                front_c(t)
                front_dt(t)
                front_poly(t, 0)
                front_poly(t, 1)
                front_ct_keep(t)
                front_delta(t)
                front_dx(t)

            def body(t, more):
                prev, nxt = t.shift(-1), t.shift(1)
                log_decay(t, 0)
                log_decay(t, 1)
                log_decay(t, 2)
                source_of(t, 0)
                for s in range(NS):
                    if s > 0:
                        term_of(t, s - 1)
                    if s + 3 <= NS:
                        log_decay(t, s + 3)
                    if s + 1 < NS:
                        source_of(t, s + 1)
                    if prev is not None:
                        if s == 0:
                            end_h(prev)
                        if s == 1:
                            end_flag(prev)
                        if s == 2:
                            end_y(prev, 0)
                        if s == 3:
                            end_y(prev, 1)
                            end_gate(prev)
                        if s == 7:
                            end_moments(prev)
                        if s == 9:
                            end_norm(prev)
                            end_quantise(prev)
                        if s == 12:
                            end_out(prev)
                    if more:
                        if s == 0:
                            front_moments(nxt)
                            front_norm(nxt)
                        if s == 4:
                            front_halo(nxt)
                        if s in (5, 6, 7, 8):
                            front_conv(nxt, 8 - s)
                        if s == 10:
                            front_c(nxt)
                            front_dt(nxt)
                        if s == 12:
                            front_poly(nxt, 0)
                        if s == 13:
                            front_poly(nxt, 1)
                            front_ct_keep(nxt)
                        if s == 14:
                            front_delta(nxt)
                        if s == 15:
                            front_dx(nxt)
                term_of(t, NS - 1)
                term_of(t, NS)
                with dve.If(other_carries(dve, t)):
                    dve.wait_ge(front_dve, at(FRONT_DVE, t, "ct_keep"))
                    for slot in range(NS + 1, SLOTS):
                        log_decay(t, slot)
                        s = slot - NS
                        if s > 2:
                            dve.wait_ge(state_ready, slot_at(t, slot - 2, 2))
                        nc.vector.tensor_scalar(csel[:, s % 2, :], ctk[t.parity][:, :], ident[0:NS, s:s + 1], None,
                                                ALU.mult).then_inc(csel_ready, 1)
                        term_of(t, slot)
                with dve.Else():
                    dve.wait_ge(logdec_ready, slot_at(t, NS))
                    dve.sem_inc(logdec_ready, NS - 1)
                    dve.wait_ge(term_ready, slot_at(t, NS, 2))
                    dve.sem_inc(term_ready, 2 * (NS - 1))
                    dve.sem_inc(csel_ready, NS - 1)

            def end(t):
                end_h(t)
                end_flag(t)
                end_y(t, 0)
                end_y(t, 1)
                end_gate(t)
                end_moments(t)
                end_norm(t)
                end_quantise(t)
                end_out(t)

            whole(dve, front, body, end)


def kernel(L0_attn_x, L0_attn_in_proj_w, L0_attn_conv_w, L0_attn_conv_b, L0_attn_x_proj_w, L0_attn_dt_w,
           L0_attn_dt_b, L0_attn_A_log, L0_attn_D_param, L0_attn_out_proj_w, L0_ffn_rhs):
    from concourse import bacc
    from concourse.bass_utils import run_bass_kernel_spmd

    def laid(a, shape=None):
        a = np.ascontiguousarray(a)
        return a if shape is None else a.reshape(shape)

    arrays = {
        "in_x": laid(L0_attn_x, (BATCH * SEQ, D)),
        "in_w_in": laid(np.asarray(L0_attn_in_proj_w).T),
        "in_conv_w": laid(L0_attn_conv_w, (DI, TAPS)),
        "in_conv_b": laid(np.asarray(L0_attn_conv_b).reshape(KI, P).T),
        "in_w_x": laid(np.asarray(L0_attn_x_proj_w).T),
        "in_dt_w": laid(L0_attn_dt_w, (DI,)),
        "in_dt_b": laid(L0_attn_dt_b),
        "in_a_log": laid(L0_attn_A_log),
        "in_d_skip": laid(L0_attn_D_param),
        "in_w_out": laid(np.asarray(L0_attn_out_proj_w).T),
        "in_rhs_t": laid(np.asarray(L0_ffn_rhs).T),
    }
    nc = bacc.Bacc("TRN2", target_bir_lowering=False, num_devices=1)
    args = [nc.dram_tensor(name, a.shape, F32, kind="ExternalInput").ap() for name, a in arrays.items()]
    out = nc.dram_tensor("out_x", (BATCH * SEQ, D), F32, kind="ExternalOutput").ap()
    mamba_block(nc, *args, out)
    result = run_bass_kernel_spmd(nc, [arrays], core_ids=[0])
    return result.results[0]["out_x"].reshape(BATCH, SEQ, D)
```

```python
from contextlib import ExitStack

import numpy as np
import concourse.bass as bass
from concourse import mybir

F32 = mybir.dt.float32
BF16 = mybir.dt.bfloat16
U32 = mybir.dt.uint32
I32 = mybir.dt.int32
ALU = mybir.AluOpType
ACT = mybir.ActivationFunctionType
AX = mybir.AxisListType

P = 128
BATCH, SEQ, D = 8, 1024, 512
DI = 1024
NS = 16
TAPS = 4
KD, KI = D // P, DI // P
HALF = 512
CHUNKS = SEQ // P
TILES = BATCH * CHUNKS
PAIRS = TILES // 2
PARITY_ROWS = TILES // 2 * P
NPROJ = 2 * NS + 1
EPS = 1e-10
LN_EPS = float(np.log(np.float32(EPS)))
NORM_EPS = 1e-5
INT8_MAX = 127.0
RSQRT_MAGIC = 1597463007.0
ROUND = 12582912.0
SMALL = 2.0 ** -5
RING = 4
SLOTS = NS + 1

FRONT_DVE = ("stats", "mean_var", "var_eps", "guess", "square1", "rstd1", "square2", "rstd2", "square3", "rstd3", "rstd",
             "xn", "halo_in", "tap3", "tap2",
             "tap1", "tap0", "halo_out", "b_rows", "c_rows", "c_last", "dt_lin", "dt_pos", "dt_negabs",
             "poly1", "poly2", "poly3", "poly4", "small", "select", "delta", "dx", "ct_keep")
FRONT_ACT = ("xnT", "xi0", "xi1", "xiT0", "xiT1", "z0", "z1", "xcT", "proj", "exp_dt",
             "xc0", "ln1p", "xc1", "ct")
FRONT_PE = ("xnT", "xi0", "xi1", "xiT0", "xiT1", "z0", "z1", "proj", "xc0", "xc1", "ct")
FRONT_POOL = ("skip",)
END_DVE = ("h", "habs", "hsel", "y0", "y1", "gate", "x2", "stats", "mean_var", "var_eps", "guess",
           "square1", "rstd1", "square2", "rstd2", "square3", "rstd3", "rstd", "xn2", "amax", "scale", "inv", "q_rounded", "q", "scaled", "out", "flag")
END_ACT = ("yT0", "yT1", "qT")
END_PE = ("fix0", "fix1", "yT0", "yT1", "attn", "qT", "ffn", "flag")


class Tile:

    def __init__(self, p, parity):
        self.p, self.parity = p, parity
        self.n = 2 * p + parity

    def shift(self, by):
        q = self.parity + by
        p = self.p + q // 2
        return None if isinstance(p, int) and p < 0 else Tile(p, q % 2)

    def row(self):
        return self.parity * PARITY_ROWS + self.p * P


def at(steps, tile, name):
    return tile.n * len(steps) + steps.index(name) + 1


def last_tile(tile):
    return isinstance(tile.n, int) and tile.n == TILES - 1


def slot_at(tile, slot, signals=1, slots=SLOTS):
    return tile.n * (slots * signals) + (slot + 1) * signals


def ring2(tile, slot):
    return (tile.parity + slot) % 2


def two_before(tile, slot):
    return (tile, slot - 2) if slot >= 2 else (tile.shift(-1), SLOTS - 2 + slot)


def decay_ring(slot):
    return 2 if slot == NS else slot % RING


def decay_before(tile, slot):
    if slot == NS:
        return tile, 14
    if slot >= RING:
        return tile, slot - RING
    return tile.shift(-1), (12, 13, NS, 15)[slot]


def mamba_block(nc, x, w_in, conv_w, conv_b, w_x, dt_w, dt_b, a_log, d_skip, w_out, rhs_t, out):
    with ExitStack() as ctx:
        def sb(name, shape, dt=F32):
            return ctx.enter_context(nc.sbuf_tensor(name, shape, dt))

        def ps(name, shape, dt=F32):
            return ctx.enter_context(nc.psum_tensor(name, shape, dt))

        def sem(name):
            return ctx.enter_context(nc.semaphore(name))

        win = sb("win", [P, KD, 2 * DI])
        wout = sb("wout", [P, KI, D])
        wx = sb("wx", [P, KI, NPROJ])
        cw = sb("cw", [P, KI, TAPS])
        cb = sb("cb", [P, KI])
        dtw = sb("dtw", [P, DI])
        dtb = sb("dtb", [P, DI])
        dskip = sb("dskip", [P, DI])
        neg_a = sb("neg_a", [P, NS])
        ident = sb("ident", [P, P])
        ident_bf = sb("ident_bf", [P, P], BF16)
        tri_before = sb("tri_before", [P, P])
        tri_upto = sb("tri_upto", [P, P])
        ones = sb("ones", [P, P])
        not_last = sb("not_last", [P, 1])
        not_first = sb("not_first", [P, 1])
        keep = sb("keep", [P, PAIRS])
        rq = sb("rq", [P, KD, D], BF16)
        rscale = sb("rscale", [P, D])
        rcol = sb("rcol", [P, KD])
        rinv = sb("rinv", [P, KD])

        xt = sb("xt", [P, D])
        fstat = sb("fstat", [P, 6])
        fmv = sb("fmv", [P, 2])
        fsmall = sb("fsmall", [P, 6])
        xn = sb("xn", [P, D])
        xnT = sb("xnT", [P, KD, P])
        xi = sb("xi", [P, DI])
        xiT = sb("xiT", [P, KI, TAPS - 1 + P])
        xc = xiT[:, :, :].rearrange("p k t -> p (k t)")[:, 0:DI]
        halo = [sb(f"halo{i}", [P, KI, TAPS - 1]) for i in range(2)]
        conv = sb("conv", [P, KI, P])
        xcT = sb("xcT", [P, KI, P])
        proj = sb("proj", [P, NPROJ])
        clast = sb("clast", [P, NS])
        dt_a = sb("dt_a", [P, DI])
        dt_pos = sb("dt_pos", [P, DI])
        dt_y = xi
        dt_poly = conv[:, :, :].rearrange("p k t -> p (k t)")
        gate = [sb(f"gate{i}", [P, DI]) for i in range(2)]
        crow = [sb(f"crow{i}", [P, NS]) for i in range(2)]
        ct = [sb(f"ct{i}", [NS, 2, P]) for i in range(2)]
        ctk = [sb(f"ctk{i}", [NS, P]) for i in range(2)]
        brow = [sb(f"brow{i}", [P, NS]) for i in range(2)]
        bmat = [sb(f"bmat{i}", [P, P]) for i in range(2)]
        delta = [sb(f"delta{i}", [P, DI]) for i in range(2)]
        dx = [sb(f"dx{i}", [P, DI]) for i in range(2)]

        logdec = [sb(f"logdec{i}", [P, DI]) for i in range(2)]
        growths = sb("growths", [P, RING, DI])
        growth = [growths[:, i, :] for i in range(RING)]
        decay = [sb(f"decay{i}", [P, DI]) for i in range(RING)]
        source = growth
        term = [sb(f"term{i}", [P, DI]) for i in range(2)]
        acc = [sb(f"acc{i}", [P, DI]) for i in range(2)]
        hmain = sb("hmain", [NS, DI])
        hcarry = sb("hcarry", [NS, DI])
        hend = [sb(f"hend{i}", [NS, DI]) for i in range(2)]
        csel = sb("csel", [NS, P])
        carried = dt_poly

        xres = sb("xres", [P, D])
        hm = sb("hm", [NS, 2])
        flag = sb("flag", [1, 2], I32)
        yg = dt_a
        ygT = dt_pos[:, :].rearrange("p (k t) -> p k t", t=P)
        x2 = sb("x2", [P, D])
        estat = sb("estat", [P, 6])
        emv = sb("emv", [P, 2])
        esmall = sb("esmall", [P, 8])
        xn2 = xn
        q_bf = sb("q_bf", [P, D], BF16)
        qT = sb("qT", [P, KD, P], BF16)
        res = xres
        rhs_sb = growths[:, 0:2, :].rearrange("p a (b n) -> p (a b) n", n=D)
        rq_rows = dt_a[:, :].bitcast(BF16).rearrange("p (k n) -> p k n", k=KD)

        cum = [ps(f"cum{i}", [P, DI]) for i in range(2)]
        state = [ps(f"state{i}", [P, HALF]) for i in range(2)]
        fbank = ps("fbank", [P, HALF])
        ebank = ps("ebank", [P, HALF])

        weights_loaded = sem("weights_loaded")
        consts_pool = sem("consts_pool")
        consts_dve = sem("consts_dve")
        consts_act = sem("consts_act")
        consts_pe = sem("consts_pe")
        x_loaded = sem("x_loaded")
        front_dve = sem("front_dve")
        front_act = sem("front_act")
        front_pe = sem("front_pe")
        front_pool = sem("front_pool")
        end_dve = sem("end_dve")
        end_act = sem("end_act")
        end_pe = sem("end_pe")
        hcarry_zeroed = sem("hcarry_zeroed")
        residual_loaded = sem("residual_loaded")
        out_stored = sem("out_stored")
        logdec_ready = sem("logdec_ready")
        cum_ready = sem("cum_ready")
        clamped = sem("clamped")
        growth_ready = sem("growth_ready")
        decay_ready = sem("decay_ready")
        source_ready = sem("source_ready")
        state_ready = sem("state_ready")
        term_ready = sem("term_ready")
        term_added = sem("term_added")
        carry_logs = sem("carry_logs")
        carry_sums = sem("carry_sums")
        carry_decays = sem("carry_decays")
        carry_products = sem("carry_products")
        carry_terms = sem("carry_terms")
        carry_added = sem("carry_added")
        carry_saved = sem("carry_saved")
        last_saved = [sem(f"last_saved{i}") for i in range(2)]
        stood = sem("stood")

        N_WEIGHTS = 11

        def saved_at(tile, slot):
            return 16 * (SLOTS * tile.p + (SLOTS * tile.parity + slot) // 2 + 1)

        def wait_saved(eng, tile, slot):
            eng.wait_ge(last_saved[ring2(tile, slot)], saved_at(tile, slot))

        def carry_at(tile, s=NS - 1):
            return (NS - 1) * tile.n + s

        def skip_carries(eng, t, s, by=1):
            if not (isinstance(t.n, int) and t.n == 0):
                eng.wait_ge(s, by * (NS - 1) * t.n)
            eng.sem_inc(s, by * (NS - 1))

        rdiags = [dt_y[:, j * P:(j + 1) * P] for j in range(KD)]

        def stand(eng):
            eng.sem_inc(stood, 1)

        def other_carries(eng, t):
            before = t.shift(-2)
            if before is None:
                eng.wait_ge(consts_pool, 1)
            else:
                eng.wait_ge(end_dve, at(END_DVE, before, "flag"))
            stand(eng)
            return eng.value_load(flag[0:1, t.parity:t.parity + 1], min_val=0, max_val=1)

        block = ctx.enter_context(nc.Block())

        def whole(tiles_of, front, body, end):
            front(Tile(0, 0))
            body(Tile(0, 0), True)
            body(Tile(0, 1), True)
            with tiles_of.Fori(1, PAIRS - 1) as p:
                body(Tile(p, 0), True)
                body(Tile(p, 1), True)
            body(Tile(PAIRS - 1, 0), True)
            body(Tile(PAIRS - 1, 1), False)
            end(Tile(PAIRS - 1, 1))

        @block.sync
        def _(sp):
            sp.dma_start(cw[:, :, :], conv_w.rearrange("(k p) t -> p k t", p=P)).then_inc(weights_loaded, 16)
            sp.dma_start(cb[:, :], conv_b).then_inc(weights_loaded, 16)
            sp.dma_start(neg_a[:, :], a_log.partition_broadcast(P)).then_inc(weights_loaded, 16)
            sp.dma_start(win[:, :, 0:DI], w_in.rearrange("(k p) e -> p k e", p=P)[:, :, 0:DI]).then_inc(weights_loaded, 16)
            sp.dma_start(win[:, :, DI:], w_in.rearrange("(k p) e -> p k e", p=P)[:, :, DI:]).then_inc(weights_loaded, 16)
            sp.dma_start(wx[:, :, :], w_x.rearrange("(k p) j -> p k j", p=P)).then_inc(weights_loaded, 16)
            sp.dma_start(dtw[:, :], dt_w.partition_broadcast(P)).then_inc(weights_loaded, 16)
            sp.dma_start(dtb[:, :], dt_b.partition_broadcast(P)).then_inc(weights_loaded, 16)
            sp.dma_start(dskip[:, :], d_skip.partition_broadcast(P)).then_inc(weights_loaded, 16)
            sp.dma_start(wout[:, :, :], w_out.rearrange("(k p) n -> p k n", p=P)).then_inc(weights_loaded, 16)
            sp.dma_start(rhs_sb, rhs_t.rearrange("(k p) n -> p k n", p=P)).then_inc(weights_loaded, 16)

            def load_x(t):
                before = t.shift(-1)
                if before is not None:
                    sp.wait_ge(front_dve, at(FRONT_DVE, before, "xn"))
                stand(sp)
                sp.dma_start(xt[:, :], x[bass.ds(t.row(), P), :]).then_inc(x_loaded, 16)

            def load_residual(t):
                before = t.shift(-1)
                if before is not None:
                    sp.wait_ge(out_stored, 16 * t.n)
                stand(sp)
                sp.dma_start(xres[:, :], x[bass.ds(t.row(), P), :]).then_inc(residual_loaded, 16)

            def store(t):
                sp.wait_ge(end_dve, at(END_DVE, t, "out"))
                stand(sp)
                sp.dma_start(out[bass.ds(t.row(), P), :], res[:, :]).then_inc(out_stored, 16)

            def save_last(t, slot):
                before = t.shift(-1)
                if slot == 0 and before is not None:
                    sp.wait_ge(end_dve, at(END_DVE, before, "h"))
                if slot == NS and before is not None:
                    sp.wait_ge(hcarry_zeroed, t.n + 1)
                if slot == NS and before is None:
                    sp.wait_ge(hcarry_zeroed, 1)
                if slot in (0, NS):
                    stand(sp)
                sp.wait_ge(term_ready, slot_at(t, slot, 2))
                rows = hmain if slot < NS else hcarry
                s = slot % NS
                sp.dma_start(rows[s:s + 1, :], term[ring2(t, slot)][P - 1:P, :]).then_inc(last_saved[ring2(t, slot)], 16)

            def finish(t):
                save_last(t, NS)
                with sp.If(other_carries(sp, t)):
                    for s in range(1, NS):
                        sp.wait_ge(carry_terms, carry_at(t, s))
                        sp.dma_start(hcarry[s:s + 1, :], carried[P - 1:P, :]).then_inc(carry_saved, 16)
                with sp.Else():
                    skip_carries(sp, t, carry_saved, 16)

            def body(t, more):
                prev = t.shift(-1)
                if prev is not None:
                    load_residual(prev)
                    finish(prev)
                if more and not (isinstance(t.p, int) and t.p == PAIRS - 1):
                    load_x(t.shift(2))
                for s in range(NS):
                    save_last(t, s)
                    if s == 12 and prev is not None:
                        store(prev)

            load_x(Tile(0, 0))
            load_x(Tile(0, 1))
            whole(sp, lambda t: None, body, lambda t: (load_residual(t), finish(t), store(t)))
            sp.wait_ge(out_stored, 16 * TILES)

        @block.gpsimd
        def _(pool):
            nc.gpsimd.memset(flag[:, :], 0)
            nc.gpsimd.memset(ones[:, :], 1.0)
            nc.gpsimd.memset(ident[:, :], 0.0)
            nc.gpsimd.memset(hcarry[:, :], 0.0).then_inc(hcarry_zeroed, 1)
            for h in (*halo,):
                nc.gpsimd.memset(h[:, :, :], 0.0)
            for h in (*hend,):
                nc.gpsimd.memset(h[:, :], 0.0)
            nc.gpsimd.memset(keep[:, :], 1.0).then_inc(consts_pool, 1)
            pool.wait_ge(consts_pool, 1)
            nc.gpsimd.memset(keep[:, 0:PAIRS:CHUNKS], 0.0)
            nc.gpsimd.affine_select(out=ident[:, :], in_=ident[:, :], compare_op=ALU.not_equal, fill=1.0, base=0,
                                    pattern=[[-1, P]], channel_multiplier=1)
            nc.gpsimd.affine_select(out=tri_before[:, :], in_=ones[:, :], compare_op=ALU.is_gt, fill=0.0, base=0,
                                    pattern=[[1, P]], channel_multiplier=-1)
            nc.gpsimd.affine_select(out=tri_upto[:, :], in_=ones[:, :], compare_op=ALU.is_ge, fill=0.0, base=0,
                                    pattern=[[1, P]], channel_multiplier=-1).then_inc(consts_pool, 1)
            pool.wait_ge(consts_pool, 2)

            def front_skip(t):
                prev = t.shift(-2)
                pool.wait_ge(front_act, at(FRONT_ACT, t, "xc1"))
                if prev is not None:
                    pool.wait_ge(end_dve, at(END_DVE, prev, "y1"))
                nc.gpsimd.tensor_tensor(acc[t.parity][:, :], xc[:, :], dskip[:, :], ALU.mult).then_inc(front_pool, 1)

            def add(t, slot):
                pool.wait_ge(term_ready, slot_at(t, slot, 2))
                if slot == 0:
                    pool.wait_ge(front_pool, at(FRONT_POOL, t, "skip"))
                else:
                    pool.wait_ge(term_added, slot_at(t, slot - 1))
                a = acc[t.parity][:, :]
                nc.gpsimd.tensor_tensor(a, a, term[ring2(t, slot)][:, :], ALU.add).then_inc(term_added, 1)

            def finish(t):
                add(t, NS)
                with pool.If(other_carries(pool, t)):
                    a = acc[t.parity][:, :]
                    pool.wait_ge(term_added, slot_at(t, NS))
                    for s in range(1, NS):
                        pool.wait_ge(carry_terms, carry_at(t, s))
                        if s > 1:
                            pool.wait_ge(carry_added, carry_at(t, s - 1))
                        stand(pool)
                        nc.gpsimd.tensor_tensor(a, a, carried[:, :], ALU.add).then_inc(carry_added, 1)
                with pool.Else():
                    skip_carries(pool, t, carry_added)

            def body(t, more):
                prev = t.shift(-1)
                if prev is not None:
                    finish(prev)
                for s in range(NS):
                    add(t, s)
                    if s == 1 and prev is not None:
                        pool.wait_ge(end_dve, at(END_DVE, prev, "h"))
                        stand(pool)
                        nc.gpsimd.memset(hcarry[:, :], 0.0).then_inc(hcarry_zeroed, 1)
                    if s == 12 and more:
                        front_skip(t.shift(1))

            whole(pool, front_skip, body, finish)

        @block.scalar
        def _(act):
            act.wait_ge(weights_loaded, 16 * N_WEIGHTS)
            nc.scalar.activation(neg_a[:, :], neg_a[:, :], ACT.Exp).then_inc(consts_act, 1)
            for k in range(KD):
                act.wait_ge(consts_pe, k + 1)
                nc.scalar.activation(rq[:, k, :], fbank[:, 0:D // 2].bitcast(BF16), ACT.Copy).then_inc(consts_act, 1)
            act.wait_ge(consts_pe, KD + 1)
            nc.scalar.activation(rscale[:, :], ebank[:, :], ACT.Copy).then_inc(consts_act, 1)

            def evacuate(t, name, dst, src=None, func=ACT.Copy):
                act.wait_ge(front_pe, at(FRONT_PE, t, name))
                src = fbank[:, :] if src is None else src
                nc.scalar.activation(dst, src, func).then_inc(front_act, 1)

            blocks4 = fbank[:, :].rearrange("p (k t) -> p k t", t=P)

            def front_xnT(t):
                prev = t.shift(-1)
                if prev is not None:
                    act.wait_ge(front_pe, at(FRONT_PE, prev, "z1"))
                evacuate(t, "xnT", xnT[:, :, :], blocks4)

            def front_xi(t, h):
                prev = t.shift(-1)
                if prev is not None:
                    act.wait_ge(front_pe, at(FRONT_PE, prev, "xiT1"))
                    act.wait_ge(front_dve, at(FRONT_DVE, prev, "select"))
                evacuate(t, f"xi{h}", xi[:, h * HALF:(h + 1) * HALF])

            def front_xiT(t, h):
                prev = t.shift(-1)
                if prev is not None:
                    act.wait_ge(front_dve, at(FRONT_DVE, prev, "dx"))
                    act.wait_ge(front_pool, at(FRONT_POOL, prev, "skip"))
                evacuate(t, f"xiT{h}", xiT[:, 4 * h:4 * h + 4, TAPS - 1:], blocks4)

            def front_gate(t, h):
                prev = t.shift(-2)
                if prev is not None:
                    act.wait_ge(end_dve, at(END_DVE, prev, "gate"))
                evacuate(t, f"z{h}", gate[t.parity][:, h * HALF:(h + 1) * HALF], func=ACT.Silu)

            def front_xcT(t):
                prev = t.shift(-1)
                if prev is not None:
                    act.wait_ge(front_pe, at(FRONT_PE, prev, "xc1"))
                act.wait_ge(front_dve, at(FRONT_DVE, t, "tap0"))
                nc.scalar.activation(xcT[:, :, :], conv[:, :, :], ACT.Silu).then_inc(front_act, 1)

            def front_proj(t):
                prev = t.shift(-1)
                if prev is not None:
                    act.wait_ge(front_dve, at(FRONT_DVE, prev, "dt_lin"))
                evacuate(t, "proj", proj[:, :], fbank[:, 0:NPROJ])

            def front_xc(t, h):
                act.wait_ge(front_dve, at(FRONT_DVE, t, "halo_out"))
                evacuate(t, f"xc{h}", xc[:, h * HALF:(h + 1) * HALF])

            def front_ct(t):
                prev = t.shift(-2)
                if prev is not None:
                    act.wait_ge(end_pe, at(END_PE, prev, "fix1"))
                evacuate(t, "ct", ct[t.parity][:, :, :], fbank[0:NS, 0:2 * P].rearrange("s (a t) -> s a t", a=2))

            def front_exp_dt(t):
                act.wait_ge(front_dve, at(FRONT_DVE, t, "dt_negabs"))
                nc.scalar.activation(dt_y[:, :], dt_a[:, :], ACT.Exp).then_inc(front_act, 1)

            def front_ln1p(t):
                act.wait_ge(front_act, at(FRONT_ACT, t, "exp_dt"))
                nc.scalar.activation(dt_a[:, :], dt_y[:, :], ACT.Ln, bias=1.0).then_inc(front_act, 1)

            def end_yT(t, h):
                act.wait_ge(end_pe, at(END_PE, t, f"yT{h}"))
                ahead = t if last_tile(t) else t.shift(1)
                act.wait_ge(front_dve, at(FRONT_DVE, ahead, "delta"))
                nc.scalar.activation(ygT[:, 4 * h:4 * h + 4, :], ebank[:, :].rearrange("p (k t) -> p k t", t=P),
                                     ACT.Copy).then_inc(end_act, 1)

            def end_qT(t):
                act.wait_ge(end_pe, at(END_PE, t, "qT"))
                nc.scalar.activation(qT[:, :, :], ebank[:, 0:D // 2].bitcast(BF16).rearrange("p (k t) -> p k t", t=P),
                                     ACT.Copy).then_inc(end_act, 1)

            def exps(t, slot):
                act.wait_ge(cum_ready, slot_at(t, slot))
                c = cum[ring2(t, slot)][:, :]
                g = growth[slot % RING][:, :]
                if slot < NS:
                    if slot >= RING:
                        act.wait_ge(state_ready, slot_at(t, slot - RING, 2))
                    elif t.shift(-1) is not None:
                        act.wait_ge(state_ready, slot_at(t.shift(-1), NS - RING + slot, 2))
                    nc.scalar.activation(g, c, ACT.Relu, bias=-LN_EPS).then_inc(clamped, 1)
                before, old = decay_before(t, slot)
                if before is not None:
                    act.wait_ge(term_ready, slot_at(before, old, 2))
                nc.scalar.activation(decay[decay_ring(slot)][:, :], c, ACT.Exp).then_inc(decay_ready, 1)
                if slot < NS:
                    act.wait_ge(clamped, slot_at(t, slot, slots=NS))
                    nc.scalar.activation(g, g, ACT.Exp, scale=-1.0, bias=-LN_EPS).then_inc(growth_ready, 1)

            def front(t):
                front_xnT(t)
                front_xi(t, 0)
                front_xi(t, 1)
                front_xiT(t, 0)
                front_xiT(t, 1)
                front_gate(t, 0)
                front_gate(t, 1)
                front_xcT(t)
                front_proj(t)
                front_exp_dt(t)
                front_xc(t, 0)
                front_ln1p(t)
                front_xc(t, 1)
                front_ct(t)

            def finish(t):
                with act.If(other_carries(act, t)):
                    for s in range(1, NS):
                        act.wait_ge(carry_sums, carry_at(t, s))
                        nc.scalar.activation(carried[:, 0:HALF], fbank[:, :], ACT.Exp)
                        nc.scalar.activation(carried[:, HALF:DI], ebank[:, :], ACT.Exp).then_inc(carry_decays, 1)
                with act.Else():
                    skip_carries(act, t, carry_decays)

            def body(t, more):
                prev, nxt = t.shift(-1), t.shift(1)
                if prev is None:
                    exps(t, 0)
                    exps(t, 1)
                for s in range(SLOTS):
                    if s + 2 < SLOTS:
                        exps(t, s + 2)
                    elif more:
                        exps(nxt, s + 2 - SLOTS)
                    if s == 0 and prev is not None:
                        finish(prev)
                    if prev is not None:
                        if s == 4:
                            end_yT(prev, 0)
                        if s == 5:
                            end_yT(prev, 1)
                        if s == 10:
                            end_qT(prev)
                    if more:
                        if s == 1:
                            front_xnT(nxt)
                        if s == 2:
                            front_xi(nxt, 0)
                        if s == 3:
                            front_xi(nxt, 1)
                        if s == 4:
                            front_xiT(nxt, 0)
                        if s == 5:
                            front_xiT(nxt, 1)
                        if s == 7:
                            front_gate(nxt, 0)
                        if s == 9:
                            front_gate(nxt, 1)
                            front_xcT(nxt)
                        if s == 10:
                            front_proj(nxt)
                        if s == 11:
                            front_exp_dt(nxt)
                            front_xc(nxt, 0)
                            front_ln1p(nxt)
                        if s == 12:
                            front_xc(nxt, 1)
                        if s == 14:
                            front_ct(nxt)

            def end(t):
                finish(t)
                end_yT(t, 0)
                end_yT(t, 1)
                end_qT(t)

            whole(act, front, body, end)

        @block.tensor
        def _(pe):
            pe.wait_ge(consts_pool, 2)
            pe.wait_ge(consts_dve, 6)
            for k in range(KD):
                if k > 0:
                    pe.wait_ge(consts_act, k + 1)
                turned = fbank[:, 0:D // 2].bitcast(BF16)
                for j in range(KD):
                    last = nc.tensor.transpose(turned[:, j * P:(j + 1) * P], rq_rows[:, j, k * P:(k + 1) * P], ident_bf[:, :])
                last.then_inc(consts_pe, 1)
            for j in range(KD):
                pe.wait_ge(consts_dve, 7 + j)
                last = nc.tensor.matmul(ebank[:, j * P:(j + 1) * P], ones[:, :], rdiags[j], start=True, stop=True)
            last.then_inc(consts_pe, 1)
            pe.wait_ge(consts_act, KD + 2)

            def front_free(t, name):
                k = FRONT_PE.index(name)
                if k > 0:
                    pe.wait_ge(front_act, at(FRONT_ACT, t, FRONT_PE[k - 1]))
                elif t.shift(-1) is not None:
                    pe.wait_ge(front_act, at(FRONT_ACT, t.shift(-1), FRONT_PE[-1]))

            def turn4(t, name, src):
                front_free(t, name)
                for j in range(4):
                    last = nc.tensor.transpose(fbank[:, j * P:(j + 1) * P], src(j), ident[:, :])
                last.then_inc(front_pe, 1)

            def front_xnT(t):
                pe.wait_ge(front_dve, at(FRONT_DVE, t, "xn"))
                turn4(t, "xnT", lambda j: xn[:, j * P:(j + 1) * P])

            def front_in(t, name, col):
                pe.wait_ge(front_act, at(FRONT_ACT, t, "xnT"))
                front_free(t, name)
                for k in range(KD):
                    last = nc.tensor.matmul(fbank[:, :], xnT[:, k, :], win[:, k, col:col + HALF], start=(k == 0), stop=(k == KD - 1))
                last.then_inc(front_pe, 1)

            def front_xiT(t, h):
                pe.wait_ge(front_act, at(FRONT_ACT, t, "xi1"))
                turn4(t, f"xiT{h}", lambda j: xi[:, (4 * h + j) * P:(4 * h + j + 1) * P])

            def front_proj(t):
                pe.wait_ge(front_act, at(FRONT_ACT, t, "xcT"))
                front_free(t, "proj")
                for k in range(KI):
                    last = nc.tensor.matmul(fbank[:, 0:NPROJ], xcT[:, k, :], wx[:, k, :], start=(k == 0), stop=(k == KI - 1))
                last.then_inc(front_pe, 1)

            def front_xc(t, h):
                turn4(t, f"xc{h}", lambda j: xcT[:, 4 * h + j, :])

            def front_ct(t):
                front_free(t, "ct")
                pe.wait_ge(front_dve, at(FRONT_DVE, t, "c_last"))
                nc.tensor.transpose(fbank[0:NS, 0:P], crow[t.parity][:, :], ident[:, :])
                nc.tensor.transpose(fbank[0:NS, P:2 * P], clast[:, :], ident[:, :]).then_inc(front_pe, 1)

            emptied = {"flag": (end_dve, END_DVE, "flag"), "fix0": (end_dve, END_DVE, "y0"),
                       "fix1": (end_dve, END_DVE, "y1"), "yT0": (end_act, END_ACT, "yT0"),
                       "yT1": (end_act, END_ACT, "yT1"), "attn": (end_dve, END_DVE, "x2"),
                       "qT": (end_act, END_ACT, "qT"), "ffn": (end_dve, END_DVE, "scaled")}

            def end_free(t, name):
                k = END_PE.index(name)
                tile = t if k > 0 else t.shift(-1)
                if tile is not None:
                    s, steps, step = emptied[END_PE[k - 1]]
                    pe.wait_ge(s, at(steps, tile, step))

            def end_flag(t):
                pe.wait_ge(end_dve, at(END_DVE, t, "hsel"))
                end_free(t, "flag")
                stand(pe)
                nc.tensor.matmul(ebank[0:1, 0:1], hm[:, 1:2], ones[0:NS, 0:1], start=True, stop=True).then_inc(end_pe, 1)

            def end_fix(t, h):
                pe.wait_ge(end_dve, at(END_DVE, t, "h"))
                end_free(t, f"fix{h}")
                nc.tensor.matmul(ebank[:, :], ct[t.parity][:, 1, :], hend[t.parity][:, h * HALF:(h + 1) * HALF],
                                 start=True, stop=True).then_inc(end_pe, 1)

            def end_yT(t, h):
                pe.wait_ge(end_dve, at(END_DVE, t, "gate"))
                end_free(t, f"yT{h}")
                for j in range(4):
                    last = nc.tensor.transpose(ebank[:, j * P:(j + 1) * P], yg[:, (4 * h + j) * P:(4 * h + j + 1) * P], ident[:, :])
                last.then_inc(end_pe, 1)

            def end_attn(t):
                end_free(t, "attn")
                for k in range(KI):
                    last = nc.tensor.matmul(ebank[:, :], ygT[:, k, :], wout[:, k, :], start=(k == 0), stop=(k == KI - 1))
                last.then_inc(end_pe, 1)

            def end_qT(t):
                pe.wait_ge(end_dve, at(END_DVE, t, "q"))
                end_free(t, "qT")
                turned = ebank[:, 0:D // 2].bitcast(BF16)
                for j in range(KD):
                    last = nc.tensor.transpose(turned[:, j * P:(j + 1) * P], q_bf[:, j * P:(j + 1) * P], ident_bf[:, :])
                last.then_inc(end_pe, 1)

            def end_ffn(t):
                end_free(t, "ffn")
                for k in range(KD):
                    last = nc.tensor.matmul(ebank[:, :], qT[:, k, :], rq[:, k, :], start=(k == 0), stop=(k == KD - 1))
                last.then_inc(end_pe, 1)

            def cumulate(t, slot):
                pe.wait_ge(logdec_ready, slot_at(t, slot))
                before, old = two_before(t, slot)
                if before is not None:
                    pe.wait_ge(decay_ready, slot_at(before, old))
                tri, b = tri_before if slot < NS else tri_upto, ring2(t, slot)
                for h in range(2):
                    cols = slice(h * HALF, (h + 1) * HALF)
                    last = nc.tensor.matmul(cum[b][:, cols], tri[:, :], logdec[b][:, cols], start=True, stop=True)
                last.then_inc(cum_ready, 1)

            def state_free(t, slot, h):
                if slot > 0:
                    pe.wait_ge(term_ready, slot_at(t, slot - 1, 2) - 1 + h)
                elif t.shift(-1) is not None:
                    pe.wait_ge(term_ready, slot_at(t.shift(-1), SLOTS - 1, 2) - 1 + h)

            def states(t, s):
                pe.wait_ge(source_ready, slot_at(t, s, slots=NS))
                for h in range(2):
                    state_free(t, s, h)
                    nc.tensor.matmul(state[h][:, :], bmat[s % 2][:, :], source[s % RING][:, h * HALF:(h + 1) * HALF],
                                     start=True, stop=True).then_inc(state_ready, 1)

            def carry(t):
                pe.wait_ge(front_dve, at(FRONT_DVE, t, "ct_keep"))
                if t.shift(-2) is not None:
                    pe.wait_ge(end_dve, at(END_DVE, t.shift(-2), "h"))
                for h in range(2):
                    state_free(t, NS, h)
                    nc.tensor.matmul(state[h][:, :], ctk[t.parity][0:1, :], hend[t.parity][0:1, h * HALF:(h + 1) * HALF],
                                     start=True, stop=True).then_inc(state_ready, 1)

            def finish(t):
                halves = ((fbank, slice(0, HALF)), (ebank, slice(HALF, DI)))
                with pe.If(other_carries(pe, t)):
                    ahead = t if last_tile(t) else t.shift(1)
                    pe.wait_ge(front_act, at(FRONT_ACT, ahead, "ct"))
                    if t.shift(-1) is not None:
                        pe.wait_ge(end_dve, at(END_DVE, t.shift(-1), "flag"))
                    for s in range(1, NS):
                        pe.wait_ge(carry_logs, carry_at(t, s))
                        for bank, cols in halves:
                            last = nc.tensor.matmul(bank[:, :], tri_upto[:, :], carried[:, cols], start=True, stop=True)
                        last.then_inc(carry_sums, 1)
                        pe.wait_ge(carry_decays, carry_at(t, s))
                        for bank, cols in halves:
                            last = nc.tensor.matmul(bank[:, :], csel[:, :], hend[t.parity][:, cols], start=True, stop=True)
                        last.then_inc(carry_products, 1)
                    pe.wait_ge(carry_terms, carry_at(t))
                with pe.Else():
                    skip_carries(pe, t, carry_sums)
                    skip_carries(pe, t, carry_products)

            def front(t):
                front_xnT(t)
                front_in(t, "xi0", 0)
                front_in(t, "xi1", HALF)
                front_xiT(t, 0)
                front_xiT(t, 1)
                front_in(t, "z0", DI)
                front_in(t, "z1", DI + HALF)
                front_proj(t)
                front_xc(t, 0)
                front_xc(t, 1)
                front_ct(t)

            def body(t, more):
                prev, nxt = t.shift(-1), t.shift(1)
                if prev is None:
                    cumulate(t, 0)
                    cumulate(t, 1)
                for s in range(SLOTS):
                    if s + 2 < SLOTS:
                        cumulate(t, s + 2)
                    elif more:
                        cumulate(nxt, s + 2 - SLOTS)
                    if more:
                        if s == 2:
                            front_in(nxt, "xi0", 0)
                        if s == 3:
                            front_in(nxt, "xi1", HALF)
                        if s == 4:
                            front_xiT(nxt, 0)
                        if s == 5:
                            front_xiT(nxt, 1)
                        if s == 7:
                            front_in(nxt, "z0", DI)
                        if s == 8:
                            front_in(nxt, "z1", DI + HALF)
                        if s == 10:
                            front_proj(nxt)
                    if prev is not None:
                        if s == 4:
                            end_yT(prev, 0)
                        if s == 5:
                            end_yT(prev, 1)
                        if s == 6:
                            end_attn(prev)
                        if s == 10:
                            end_qT(prev)
                        if s == 11:
                            end_ffn(prev)
                    if s < NS:
                        states(t, s)
                    else:
                        carry(t)
                    if s == 0 and prev is not None:
                        finish(prev)
                    if more:
                        if s == 1:
                            front_xnT(nxt)
                        if s == 10:
                            front_xc(nxt, 0)
                        if s == 11:
                            front_xc(nxt, 1)
                        if s == 13:
                            front_ct(nxt)
                    if prev is not None:
                        if s == 12:
                            end_flag(prev)
                        if s == 1:
                            end_fix(prev, 0)
                        if s == 2:
                            end_fix(prev, 1)

            def end(t):
                finish(t)
                end_fix(t, 0)
                end_fix(t, 1)
                end_yT(t, 0)
                end_yT(t, 1)
                end_attn(t)
                end_qT(t)
                end_ffn(t)
                end_flag(t)

            whole(pe, front, body, end)

        @block.vector
        def _(dve):
            def done(ins, s, value):
                ins.then_inc(s, 1)
                dve.wait_ge(s, value)

            dve.wait_ge(consts_pool, 2)
            dve.wait_ge(weights_loaded, 16 * N_WEIGHTS)
            nc.vector.tensor_copy(ident_bf[:, :], ident[:, :])
            nc.vector.tensor_scalar(not_last[:, :], ident[:, P - 1:P], -1.0, 1.0, ALU.mult, ALU.add)
            nc.vector.tensor_scalar(not_first[:, :], ident[:, 0:1], -1.0, 1.0, ALU.mult, ALU.add)
            done(nc.vector.tensor_reduce(rcol[:, :], rhs_sb, AX.X, ALU.max, apply_absolute_value=True), consts_dve, 1)
            done(nc.vector.tensor_scalar(rcol[:, :], rcol[:, :], 1e-12, 1.0 / INT8_MAX, ALU.max, ALU.mult), consts_dve, 2)
            done(nc.vector.reciprocal(rinv[:, :], rcol[:, :]), consts_dve, 3)
            for k in range(KD):
                nc.vector.tensor_scalar(rhs_sb[:, k, :], rhs_sb[:, k, :], rinv[:, k:k + 1], ROUND, ALU.mult, ALU.add)
            nc.vector.tensor_scalar(yg[:, 0:1], ones[:, 0:1], 0.0, None, ALU.mult).then_inc(consts_dve, 1)
            dve.wait_ge(consts_dve, 4)
            nc.vector.tensor_scalar(rq_rows, rhs_sb, -ROUND, None, ALU.add).then_inc(consts_dve, 1)
            dve.wait_ge(consts_act, 1)
            nc.vector.tensor_scalar(neg_a[:, :], neg_a[:, :], -1.0, None, ALU.mult).then_inc(consts_dve, 1)
            for j in range(KD):
                nc.vector.tensor_scalar(rdiags[j], ident[:, :], rcol[:, j:j + 1], None, ALU.mult).then_inc(consts_dve, 1)
            dve.wait_ge(consts_act, KD + 2)

            def moments(t, src, stats, mv, small, s, steps):
                done(nc.vector.bn_stats(stats[:, :], src), s, at(steps, t, "stats"))
                stand(dve)
                done(nc.vector.bn_aggr(mv[:, :], stats[:, :]), s, at(steps, t, "mean_var"))
                done(nc.vector.tensor_scalar(small[:, 0:1], mv[:, 1:2], NORM_EPS, None, ALU.add), s, at(steps, t, "var_eps"))

            def norm(t, src, mv, small, dst, s, steps):
                v = small[:, 0:1]
                done(nc.vector.tensor_scalar(small[:, 1:2].bitcast(I32), v.bitcast(I32), -0.5, RSQRT_MAGIC, ALU.mult, ALU.add),
                     s, at(steps, t, "guess"))
                r, c = small[:, 1:2], 1.0
                for k in (1, 2, 3):
                    done(nc.vector.scalar_tensor_tensor(out=small[:, 2:3], in0=r, scalar=v, in1=r, op0=ALU.mult, op1=ALU.mult),
                         s, at(steps, t, f"square{k}"))
                    done(nc.vector.scalar_tensor_tensor(out=r, in0=small[:, 2:3], scalar=-3.0 * c * c, in1=r, op0=ALU.add,
                                                        op1=ALU.mult), s, at(steps, t, f"rstd{k}"))
                    c = -2.0 * c ** 3
                done(nc.vector.tensor_scalar(small[:, 3:4], r, 1.0 / c, None, ALU.mult), s, at(steps, t, "rstd"))
                nc.vector.tensor_scalar(dst, src, mv[:, 0:1], small[:, 3:4], ALU.subtract, ALU.mult).then_inc(s, 1)

            def front_moments(t):
                dve.wait_ge(x_loaded, 16 * (t.n + 1))
                moments(t, xt[:, :], fstat, fmv, fsmall, front_dve, FRONT_DVE)

            def front_norm(t):
                if t.shift(-1) is not None:
                    dve.wait_ge(front_pe, at(FRONT_PE, t.shift(-1), "xnT"))
                if t.shift(-3) is not None:
                    dve.wait_ge(end_dve, at(END_DVE, t.shift(-3), "q"))
                norm(t, xt[:, :], fmv, fsmall, xn[:, :], front_dve, FRONT_DVE)

            def front_halo(t):
                if t.shift(-1) is not None:
                    dve.wait_ge(front_dve, at(FRONT_DVE, t.shift(-1), "dx"))
                    dve.wait_ge(front_pool, at(FRONT_POOL, t.shift(-1), "skip"))
                nc.vector.tensor_scalar(xiT[:, :, 0:TAPS - 1], halo[t.parity][:, :, :], keep[:, bass.ds(t.p, 1)], None,
                                        ALU.mult).then_inc(front_dve, 1)

            def front_conv(t, tap):
                if tap == TAPS - 1:
                    dve.wait_ge(front_act, at(FRONT_ACT, t, "xiT1"))
                    if t.shift(-1) is not None:
                        dve.wait_ge(front_act, at(FRONT_ACT, t.shift(-1), "xcT"))
                    if t.shift(-2) is not None:
                        dve.wait_ge(carry_added, carry_at(t.shift(-2)))
                        dve.wait_ge(carry_saved, 16 * carry_at(t.shift(-2)))
                else:
                    dve.wait_ge(front_dve, at(FRONT_DVE, t, f"tap{tap + 1}"))
                for k in range(KI):
                    src, w = xiT[:, k, tap:tap + P], cw[:, k, tap:tap + 1]
                    if tap == TAPS - 1:
                        last = nc.vector.tensor_scalar(conv[:, k, :], src, w, cb[:, k:k + 1], ALU.mult, ALU.add)
                    else:
                        last = nc.vector.scalar_tensor_tensor(out=conv[:, k, :], in0=src, scalar=w, in1=conv[:, k, :],
                                                              op0=ALU.mult, op1=ALU.add)
                last.then_inc(front_dve, 1)
                if tap == 0:
                    nc.vector.tensor_copy(halo[t.parity][:, :, :], xiT[:, :, P:]).then_inc(front_dve, 1)

            def front_c(t):
                dve.wait_ge(front_act, at(FRONT_ACT, t, "proj"))
                if t.shift(-2) is not None:
                    dve.wait_ge(term_ready, slot_at(t.shift(-2), NS - 1, 2))
                    dve.wait_ge(front_pe, at(FRONT_PE, t.shift(-1), "ct"))
                elif t.shift(-1) is not None:
                    dve.wait_ge(front_pe, at(FRONT_PE, t.shift(-1), "ct"))
                nc.vector.tensor_copy(brow[t.parity][:, :], proj[:, 1:1 + NS]).then_inc(front_dve, 1)
                last_row = ident[:, P - 1:P]
                c = proj[:, 1 + NS:NPROJ]
                nc.vector.tensor_scalar(crow[t.parity][:, :], c, not_last[:, :], last_row, ALU.mult, ALU.add).then_inc(front_dve, 1)
                nc.vector.tensor_scalar(clast[:, :], c, 1.0, last_row, ALU.subtract, ALU.mult).then_inc(front_dve, 1)

            def front_ct_keep(t):
                dve.wait_ge(front_act, at(FRONT_ACT, t, "ct"))
                if t.shift(-2) is not None:
                    dve.wait_ge(state_ready, slot_at(t.shift(-2), SLOTS - 1, 2))
                    dve.wait_ge(carry_terms, carry_at(t.shift(-2)))
                nc.vector.tensor_scalar(ctk[t.parity][:, :], ct[t.parity][:, 0, :], keep[0:NS, bass.ds(t.p, 1)], None,
                                        ALU.mult).then_inc(front_dve, 1)

            def front_dt(t):
                if t.shift(-2) is not None:
                    dve.wait_ge(end_pe, at(END_PE, t.shift(-2), "attn"))
                done(nc.vector.scalar_tensor_tensor(out=dt_a[:, :], in0=dtw[:, :], scalar=proj[:, 0:1], in1=dtb[:, :],
                                                    op0=ALU.mult, op1=ALU.add), front_dve, at(FRONT_DVE, t, "dt_lin"))
                done(nc.vector.tensor_scalar(dt_pos[:, :], dt_a[:, :], 0.0, None, ALU.max), front_dve, at(FRONT_DVE, t, "dt_pos"))
                nc.vector.scalar_tensor_tensor(out=dt_a[:, :], in0=dt_pos[:, :], scalar=-2.0, in1=dt_a[:, :],
                                               op0=ALU.mult, op1=ALU.add).then_inc(front_dve, 1)

            def front_poly(t, half):
                y, r = dt_y[:, :], dt_poly[:, :]
                if half == 0:
                    dve.wait_ge(front_act, at(FRONT_ACT, t, "exp_dt"))
                    done(nc.vector.tensor_scalar(r, y, -0.25, 1.0 / 3.0, ALU.mult, ALU.add), front_dve, at(FRONT_DVE, t, "poly1"))
                    nc.vector.tensor_tensor(r, r, y, ALU.mult).then_inc(front_dve, 1)
                else:
                    dve.wait_ge(front_dve, at(FRONT_DVE, t, "poly2"))
                    done(nc.vector.scalar_tensor_tensor(out=r, in0=r, scalar=-0.5, in1=y, op0=ALU.add, op1=ALU.mult),
                         front_dve, at(FRONT_DVE, t, "poly3"))
                    nc.vector.scalar_tensor_tensor(out=r, in0=r, scalar=1.0, in1=y, op0=ALU.add, op1=ALU.mult).then_inc(front_dve, 1)

            def front_delta(t):
                dve.wait_ge(front_act, at(FRONT_ACT, t, "ln1p"))
                mask = dt_y[:, :].bitcast(U32)
                nc.vector.tensor_scalar(mask, dt_y[:, :], SMALL, None, ALU.is_lt).then_inc(front_dve, 1)
                dve.wait_ge(front_dve, at(FRONT_DVE, t, "small"))
                stand(dve)
                done(nc.vector.copy_predicated(dt_a[:, :], mask, dt_poly[:, :]), front_dve, at(FRONT_DVE, t, "select"))
                if t.shift(-2) is not None:
                    dve.wait_ge(logdec_ready, slot_at(t.shift(-2), SLOTS - 1))
                    dve.wait_ge(carry_logs, carry_at(t.shift(-2)))
                done(nc.vector.tensor_tensor(delta[t.parity][:, :], dt_a[:, :], dt_pos[:, :], ALU.add),
                     front_dve, at(FRONT_DVE, t, "delta"))

            def front_dx(t):
                dve.wait_ge(front_act, at(FRONT_ACT, t, "xc1"))
                if t.shift(-2) is not None:
                    dve.wait_ge(source_ready, slot_at(t.shift(-2), NS - 1, slots=NS))
                nc.vector.tensor_tensor(dx[t.parity][:, :], delta[t.parity][:, :], xc[:, :], ALU.mult).then_inc(front_dve, 1)

            def end_h(t):
                before = t.shift(-1)
                for slot in (SLOTS - 2, SLOTS - 1):
                    wait_saved(dve, t, slot)
                dve.wait_ge(carry_saved, 16 * carry_at(t))
                dve.wait_ge(state_ready, slot_at(t, SLOTS - 1, 2))
                dve.wait_ge(carry_products, carry_at(t))
                if before is not None:
                    dve.wait_ge(end_pe, at(END_PE, before, "fix1"))
                h = hend[t.parity][:, :]
                done(nc.vector.tensor_tensor(h, hmain[:, :], hcarry[:, :], ALU.add), end_dve, at(END_DVE, t, "h"))
                done(nc.vector.tensor_reduce(hm[:, 0:1], h, AX.X, ALU.max, apply_absolute_value=True), end_dve, at(END_DVE, t, "habs"))
                nc.vector.tensor_scalar(hm[:, 1:2], hm[:, 0:1], not_first[0:NS, :], None, ALU.mult).then_inc(end_dve, 1)

            def end_flag(t):
                dve.wait_ge(carry_added, carry_at(t))
                dve.wait_ge(carry_decays, carry_at(t))
                dve.wait_ge(carry_saved, 16 * carry_at(t))
                dve.wait_ge(end_pe, at(END_PE, t, "flag"))
                after = keep[0:1, bass.ds(t.p + 1, 1)] if not (isinstance(t.p, int) and t.p == PAIRS - 1) else keep[0:1, 0:1]
                nc.vector.tensor_scalar(flag[0:1, t.parity:t.parity + 1], ebank[0:1, 0:1], after, 0.0, ALU.mult, ALU.is_gt)\
                    .then_inc(end_dve, 1)

            def end_y(t, h):
                cols = slice(h * HALF, (h + 1) * HALF)
                dve.wait_ge(term_added, slot_at(t, SLOTS - 1))
                dve.wait_ge(carry_added, carry_at(t))
                dve.wait_ge(front_dve, at(FRONT_DVE, t if last_tile(t) else t.shift(1), "delta"))
                dve.wait_ge(end_pe, at(END_PE, t, f"fix{h}"))
                nc.vector.tensor_tensor(yg[:, cols], ebank[:, :], acc[t.parity][:, cols], ALU.add).then_inc(end_dve, 1)

            def end_gate(t):
                dve.wait_ge(end_dve, at(END_DVE, t, "y1"))
                nc.vector.tensor_tensor(yg[:, :], yg[:, :], gate[t.parity][:, :], ALU.mult).then_inc(end_dve, 1)

            def end_moments(t):
                dve.wait_ge(end_pe, at(END_PE, t, "attn"))
                dve.wait_ge(residual_loaded, 16 * (t.n + 1))
                if t.shift(-1) is not None:
                    dve.wait_ge(end_dve, at(END_DVE, t.shift(-1), "out"))
                done(nc.vector.tensor_tensor(x2[:, :], ebank[:, :], xres[:, :], ALU.add), end_dve, at(END_DVE, t, "x2"))
                moments(t, x2[:, :], estat, emv, esmall, end_dve, END_DVE)

            def end_norm(t):
                if not last_tile(t) and not last_tile(t.shift(1)):
                    dve.wait_ge(front_pe, at(FRONT_PE, t.shift(2), "xnT"))
                norm(t, x2[:, :], emv, esmall, xn2[:, :], end_dve, END_DVE)

            def end_quantise(t):
                dve.wait_ge(end_dve, at(END_DVE, t, "xn2"))
                done(nc.vector.tensor_reduce(esmall[:, 6:7], xn2[:, :], AX.X, ALU.max, apply_absolute_value=True),
                     end_dve, at(END_DVE, t, "amax"))
                done(nc.vector.tensor_scalar(esmall[:, 6:7], esmall[:, 6:7], 1e-12, 1.0 / INT8_MAX, ALU.max, ALU.mult),
                     end_dve, at(END_DVE, t, "scale"))
                done(nc.vector.reciprocal(esmall[:, 7:8], esmall[:, 6:7]), end_dve, at(END_DVE, t, "inv"))
                done(nc.vector.tensor_scalar(xn2[:, :], xn2[:, :], esmall[:, 7:8], ROUND, ALU.mult, ALU.add),
                     end_dve, at(END_DVE, t, "q_rounded"))
                if t.shift(-1) is not None:
                    dve.wait_ge(end_pe, at(END_PE, t.shift(-1), "qT"))
                nc.vector.tensor_scalar(q_bf[:, :], xn2[:, :], -ROUND, None, ALU.add).then_inc(end_dve, 1)

            def end_out(t):
                dve.wait_ge(end_pe, at(END_PE, t, "ffn"))
                if t.shift(-1) is not None:
                    dve.wait_ge(out_stored, 16 * t.n)
                done(nc.vector.scalar_tensor_tensor(out=res[:, :], in0=ebank[:, :], scalar=esmall[:, 6:7], in1=rscale[:, :],
                                                    op0=ALU.mult, op1=ALU.mult), end_dve, at(END_DVE, t, "scaled"))
                nc.vector.tensor_tensor(res[:, :], res[:, :], x2[:, :], ALU.add).then_inc(end_dve, 1)

            def log_decay(t, slot):
                if slot == 0:
                    dve.wait_ge(front_dve, at(FRONT_DVE, t, "delta"))
                before, old = two_before(t, slot)
                if before is not None:
                    dve.wait_ge(cum_ready, slot_at(before, old))
                s = slot % NS
                nc.vector.tensor_scalar(logdec[ring2(t, slot)][:, :], delta[t.parity][:, :], neg_a[:, s:s + 1], LN_EPS,
                                        ALU.mult, ALU.max).then_inc(logdec_ready, 1)

            def source_of(t, s):
                if s == 0:
                    dve.wait_ge(front_dve, at(FRONT_DVE, t, "dx"))
                dve.wait_ge(growth_ready, slot_at(t, s, slots=NS))
                g = growth[s % RING][:, :]
                if s >= 2:
                    dve.wait_ge(state_ready, slot_at(t, s - 2, 2))
                elif t.shift(-1) is not None:
                    dve.wait_ge(state_ready, slot_at(t.shift(-1), NS - 2 + s, 2))
                nc.vector.tensor_scalar(bmat[s % 2][:, :], tri_upto[:, :], brow[t.parity][:, s:s + 1], None, ALU.mult)
                nc.vector.tensor_tensor(g, g, dx[t.parity][:, :], ALU.mult).then_inc(source_ready, 1)

            def term_of(t, slot):
                before, old = two_before(t, slot)
                if before is not None:
                    dve.wait_ge(term_added, slot_at(before, old))
                    wait_saved(dve, before, old)
                dve.wait_ge(decay_ready, slot_at(t, slot))
                for h in range(2):
                    cols = slice(h * HALF, (h + 1) * HALF)
                    dst, d = term[ring2(t, slot)][:, cols], decay[decay_ring(slot)][:, cols]
                    dve.wait_ge(state_ready, slot_at(t, slot, 2) - 1 + h)
                    if slot < NS:
                        nc.vector.scalar_tensor_tensor(out=dst, in0=state[h][:, :], scalar=crow[t.parity][:, slot:slot + 1], in1=d,
                                                       op0=ALU.mult, op1=ALU.mult).then_inc(term_ready, 1)
                    else:
                        nc.vector.tensor_tensor(dst, state[h][:, :], d, ALU.mult).then_inc(term_ready, 1)

            def finish(t):
                with dve.If(other_carries(dve, t)):
                    ahead = t if last_tile(t) else t.shift(1)
                    dve.wait_ge(front_dve, at(FRONT_DVE, ahead, "dx"))
                    dve.wait_ge(front_act, at(FRONT_ACT, ahead, "ct"))
                    dve.wait_ge(front_dve, at(FRONT_DVE, t, "dx"))
                    for s in range(1, NS):
                        if s > 1:
                            dve.wait_ge(carry_added, carry_at(t, s - 1))
                            dve.wait_ge(carry_saved, 16 * carry_at(t, s - 1))
                            dve.wait_ge(carry_products, carry_at(t, s - 1))
                        stand(dve)
                        nc.vector.tensor_scalar(csel[:, :], ctk[t.parity][:, :], ident[0:NS, s:s + 1], None, ALU.mult)
                        nc.vector.tensor_scalar(carried[:, :], delta[t.parity][:, :], neg_a[:, s:s + 1], LN_EPS,
                                                ALU.mult, ALU.max).then_inc(carry_logs, 1)
                        dve.wait_ge(carry_products, carry_at(t, s))
                        stand(dve)
                        nc.vector.tensor_tensor(carried[:, 0:HALF], fbank[:, :], carried[:, 0:HALF], ALU.mult)
                        nc.vector.tensor_tensor(carried[:, HALF:DI], ebank[:, :], carried[:, HALF:DI], ALU.mult)\
                            .then_inc(carry_terms, 1)
                with dve.Else():
                    skip_carries(dve, t, carry_logs)
                    skip_carries(dve, t, carry_terms)

            def front(t):
                front_moments(t)
                front_norm(t)
                front_halo(t)
                for tap in range(TAPS - 1, -1, -1):
                    front_conv(t, tap)
                front_c(t)
                front_dt(t)
                front_poly(t, 0)
                front_poly(t, 1)
                front_delta(t)
                front_dx(t)
                front_ct_keep(t)

            def body(t, more):
                prev, nxt = t.shift(-1), t.shift(1)
                if prev is None:
                    log_decay(t, 0)
                    log_decay(t, 1)
                    log_decay(t, 2)
                    source_of(t, 0)
                for s in range(SLOTS):
                    if s > 0:
                        term_of(t, s - 1)
                    elif prev is not None:
                        term_of(prev, NS)
                    if s + 3 < SLOTS:
                        log_decay(t, s + 3)
                    elif more and s > SLOTS - 3:
                        log_decay(nxt, s + 3 - SLOTS)
                    if s + 1 < NS:
                        source_of(t, s + 1)
                    elif more and s == NS:
                        source_of(nxt, 0)
                    if s == 0 and prev is not None:
                        finish(prev)
                    if prev is not None:
                        if s == 1:
                            end_h(prev)
                        if s == 13:
                            end_flag(prev)
                        if s == 2:
                            end_y(prev, 0)
                        if s == 3:
                            end_y(prev, 1)
                            end_gate(prev)
                        if s == 7:
                            end_moments(prev)
                        if s == 9:
                            end_norm(prev)
                            end_quantise(prev)
                        if s == 11:
                            end_out(prev)
                    if more:
                        if s == 0:
                            front_moments(nxt)
                            front_norm(nxt)
                        if s == 4:
                            front_halo(nxt)
                        if s in (5, 6, 7, 8):
                            front_conv(nxt, 8 - s)
                        if s == 10:
                            front_c(nxt)
                            front_dt(nxt)
                        if s == 12:
                            front_poly(nxt, 0)
                            front_poly(nxt, 1)
                        if s == 13:
                            front_delta(nxt)
                        if s == 14:
                            log_decay(nxt, 0)
                            front_dx(nxt)
                        if s == 15:
                            front_ct_keep(nxt)

            def end(t):
                term_of(t, NS)
                finish(t)
                end_h(t)
                end_y(t, 0)
                end_y(t, 1)
                end_gate(t)
                end_moments(t)
                end_norm(t)
                end_quantise(t)
                end_out(t)
                end_flag(t)

            whole(dve, front, body, end)


def kernel(L0_attn_x, L0_attn_in_proj_w, L0_attn_conv_w, L0_attn_conv_b, L0_attn_x_proj_w, L0_attn_dt_w,
           L0_attn_dt_b, L0_attn_A_log, L0_attn_D_param, L0_attn_out_proj_w, L0_ffn_rhs):
    from concourse import bacc
    from concourse.bass_utils import run_bass_kernel_spmd

    def laid(a, shape=None):
        a = np.ascontiguousarray(a)
        return a if shape is None else a.reshape(shape)

    arrays = {
        "in_x": laid(L0_attn_x, (BATCH * SEQ, D)),
        "in_w_in": laid(np.asarray(L0_attn_in_proj_w).T),
        "in_conv_w": laid(L0_attn_conv_w, (DI, TAPS)),
        "in_conv_b": laid(np.asarray(L0_attn_conv_b).reshape(KI, P).T),
        "in_w_x": laid(np.asarray(L0_attn_x_proj_w).T),
        "in_dt_w": laid(L0_attn_dt_w, (DI,)),
        "in_dt_b": laid(L0_attn_dt_b),
        "in_a_log": laid(L0_attn_A_log),
        "in_d_skip": laid(L0_attn_D_param),
        "in_w_out": laid(np.asarray(L0_attn_out_proj_w).T),
        "in_rhs_t": laid(np.asarray(L0_ffn_rhs).T),
    }
    nc = bacc.Bacc("TRN2", target_bir_lowering=False, num_devices=1)
    args = [nc.dram_tensor(name, a.shape, F32, kind="ExternalInput").ap() for name, a in arrays.items()]
    out = nc.dram_tensor("out_x", (BATCH * SEQ, D), F32, kind="ExternalOutput").ap()
    mamba_block(nc, *args, out)
    result = run_bass_kernel_spmd(nc, [arrays], core_ids=[0])
    return result.results[0]["out_x"].reshape(BATCH, SEQ, D)
```
